# Optimizing a Trainium2 kernel written in Bass

```python
import numpy as np
import jax
import jax.numpy as jnp

def _softmax(x, axis=-1):
    return jax.nn.softmax(x, axis=axis)

def _gelu(x):
    return jax.nn.gelu(x, approximate=True)

def _silu(x):
    return jax.nn.silu(x)

def _sigmoid(x):
    return jax.nn.sigmoid(x)

def _layernorm(x, axis=-1, eps=1e-05):
    m = jnp.mean(x, axis=axis, keepdims=True)
    v = jnp.var(x, axis=axis, keepdims=True)
    return (x - m) / jnp.sqrt(v + eps)

def _scatter_add(tgt, idx, src, axis=0):
    return tgt.at[idx].add(src)

def _segment_sum(src, seg, n):
    return jax.ops.segment_sum(src, seg, n)
kernel_name = 'mk_seq_postln_d1_jaxref_r4_d7de12'

def setup_inputs(seed: int=0):
    np.random.seed(seed)
    _w = jnp.asarray

    def _L0_attn_setup():
        import jax, jax.numpy as jnp
        import numpy as np
        H = 1024
        D = H // 4
        key = jax.random.key(seed)
        k1, k2, k3, k4, k5 = jax.random.split(key, 5)
        x = jax.random.normal(k1, (4, 1024, H), dtype=jnp.float32)
        s_in = 1.0 / np.sqrt(H)
        Wqkv = jax.random.normal(k2, (H, 3 * D), dtype=jnp.float32) * s_in
        bqkv = jax.random.normal(k3, (3 * D,), dtype=jnp.float32) * 0.01
        Wo = jax.random.normal(k4, (D, H), dtype=jnp.float32) * (1.0 / np.sqrt(D))
        bo = jax.random.normal(k5, (H,), dtype=jnp.float32) * 0.01
        return {'x': x, 'Wqkv': Wqkv, 'bqkv': bqkv, 'Wo': Wo, 'bo': bo}
    _L0_attn_in = _L0_attn_setup()

    def _L0_ffn_setup():
        import jax, jax.numpy as jnp
        import numpy as np
        HID = 1024
        INTER = 2752
        BITS = 4
        PACK = 8
        MAXQ = 15
        GROUP = 128

        def _dequant(qweight, scales, qzeros, g_idx):
            shifts = jnp.arange(PACK, dtype=jnp.uint32) * BITS
            qw = qweight.astype(jnp.uint32)
            w = (qw[:, None, :] >> shifts[None, :, None] & MAXQ).reshape(-1, qweight.shape[1])
            qz = qzeros.astype(jnp.uint32)
            z = ((qz[:, :, None] >> shifts[None, None, :] & MAXQ) + 1).reshape(qzeros.shape[0], -1)
            s = scales[g_idx]
            return (w.astype(scales.dtype) - z[g_idx].astype(scales.dtype)) * s
        key = jax.random.key(seed)
        ks = jax.random.split(key, 16)

        def qw(k, K, N):
            return jax.random.randint(k, (K // PACK, N), 0, 2147483647, dtype=jnp.int32)

        def qz(k, G, N):
            return jax.random.randint(k, (G, N // PACK), 0, 2147483647, dtype=jnp.int32)

        def sc(k, G, N):
            return jax.random.uniform(k, (G, N), jnp.float32, 0.001, 0.01)
        Gk = HID // GROUP
        Gd = INTER // GROUP
        return {'x': jax.random.normal(ks[0], (4, 512, HID), jnp.float32), 'gate_qweight': qw(ks[1], HID, INTER), 'gate_scales': sc(ks[2], Gk, INTER), 'gate_qzeros': qz(ks[3], Gk, INTER), 'gate_g_idx': (jnp.arange(HID) // GROUP).astype(jnp.int32), 'up_qweight': qw(ks[4], HID, INTER), 'up_scales': sc(ks[5], Gk, INTER), 'up_qzeros': qz(ks[6], Gk, INTER), 'up_g_idx': (jnp.arange(HID) // GROUP).astype(jnp.int32), 'down_qweight': qw(ks[7], INTER, HID), 'down_scales': sc(ks[8], Gd, HID), 'down_qzeros': qz(ks[9], Gd, HID), 'down_g_idx': (jnp.arange(INTER) // GROUP).astype(jnp.int32)}
    _L0_ffn_in = _L0_ffn_setup()
    _d = {'L0_attn_x': _L0_attn_in['x'], 'L0_attn_Wqkv': _L0_attn_in['Wqkv'], 'L0_attn_bqkv': _L0_attn_in['bqkv'], 'L0_attn_Wo': _L0_attn_in['Wo'], 'L0_attn_bo': _L0_attn_in['bo'], 'L0_ffn_gate_qweight': _L0_ffn_in['gate_qweight'], 'L0_ffn_gate_scales': _L0_ffn_in['gate_scales'], 'L0_ffn_gate_qzeros': _L0_ffn_in['gate_qzeros'], 'L0_ffn_gate_g_idx': _L0_ffn_in['gate_g_idx'], 'L0_ffn_up_qweight': _L0_ffn_in['up_qweight'], 'L0_ffn_up_scales': _L0_ffn_in['up_scales'], 'L0_ffn_up_qzeros': _L0_ffn_in['up_qzeros'], 'L0_ffn_up_g_idx': _L0_ffn_in['up_g_idx'], 'L0_ffn_down_qweight': _L0_ffn_in['down_qweight'], 'L0_ffn_down_scales': _L0_ffn_in['down_scales'], 'L0_ffn_down_qzeros': _L0_ffn_in['down_qzeros'], 'L0_ffn_down_g_idx': _L0_ffn_in['down_g_idx']}
    _x0 = _d['L0_attn_x']
    _d['L0_attn_x'] = jax.random.normal(jax.random.fold_in(jax.random.key(seed), 1), (1, 2048, 1024), dtype=_x0.dtype)
    del _x0
    return _d

def reference(L0_attn_x, L0_attn_Wqkv, L0_attn_bqkv, L0_attn_Wo, L0_attn_bo, L0_ffn_gate_qweight, L0_ffn_gate_scales, L0_ffn_gate_qzeros, L0_ffn_gate_g_idx, L0_ffn_up_qweight, L0_ffn_up_scales, L0_ffn_up_qzeros, L0_ffn_up_g_idx, L0_ffn_down_qweight, L0_ffn_down_scales, L0_ffn_down_qzeros, L0_ffn_down_g_idx):

    def _L0_attn_ref(x, Wqkv, bqkv, Wo, bo):
        import jax, jax.numpy as jnp
        import numpy as np
        H = 1024
        D = H // 4
        B, S, C = x.shape
        d = C // 4
        qkv = jnp.einsum('bsc,cf->bsf', x, Wqkv) + bqkv
        qkv = qkv.reshape(B, S, 3, d)
        q, k, v = (qkv[:, :, 0], qkv[:, :, 1], qkv[:, :, 2])
        scale = 1.0 / jnp.sqrt(jnp.float32(d)).astype(x.dtype)
        attn = jnp.einsum('bqd,bkd->bqk', q, k) * scale
        attn = jax.nn.softmax(attn, axis=-1)
        out = jnp.einsum('bqk,bkd->bqd', attn, v)
        return jnp.einsum('bqd,dc->bqc', out, Wo) + bo

    def _L0_ffn_ref(x, gate_qweight, gate_scales, gate_qzeros, gate_g_idx, up_qweight, up_scales, up_qzeros, up_g_idx, down_qweight, down_scales, down_qzeros, down_g_idx):
        import jax, jax.numpy as jnp
        import numpy as np
        HID = 1024
        INTER = 2752
        BITS = 4
        PACK = 8
        MAXQ = 15
        GROUP = 128

        def _dequant(qweight, scales, qzeros, g_idx):
            shifts = jnp.arange(PACK, dtype=jnp.uint32) * BITS
            qw = qweight.astype(jnp.uint32)
            w = (qw[:, None, :] >> shifts[None, :, None] & MAXQ).reshape(-1, qweight.shape[1])
            qz = qzeros.astype(jnp.uint32)
            z = ((qz[:, :, None] >> shifts[None, None, :] & MAXQ) + 1).reshape(qzeros.shape[0], -1)
            s = scales[g_idx]
            return (w.astype(scales.dtype) - z[g_idx].astype(scales.dtype)) * s
        Wg = _dequant(gate_qweight, gate_scales, gate_qzeros, gate_g_idx)
        Wu = _dequant(up_qweight, up_scales, up_qzeros, up_g_idx)
        Wd = _dequant(down_qweight, down_scales, down_qzeros, down_g_idx)
        xf = x.reshape(-1, x.shape[-1])
        h = jax.nn.silu(xf @ Wg) * (xf @ Wu)
        out = h @ Wd
        return out.reshape(x.shape[:-1] + (Wd.shape[1],))
    x = L0_attn_x
    x = _layernorm(x + _L0_attn_ref(x, L0_attn_Wqkv, L0_attn_bqkv, L0_attn_Wo, L0_attn_bo), axis=-1)
    x = _layernorm(x + _L0_ffn_ref(x, L0_ffn_gate_qweight, L0_ffn_gate_scales, L0_ffn_gate_qzeros, L0_ffn_gate_g_idx, L0_ffn_up_qweight, L0_ffn_up_scales, L0_ffn_up_qzeros, L0_ffn_up_g_idx, L0_ffn_down_qweight, L0_ffn_down_scales, L0_ffn_down_qzeros, L0_ffn_down_g_idx), axis=-1)
    return x

_drawn_inputs = setup_inputs


def setup_inputs(seed=0):
    import zlib

    import numpy as np

    out = dict(_drawn_inputs(seed))
    spreads = {}
    factors = {'L0_attn_bqkv': 4.418, 'L0_attn_bo': 4.74}
    for name, (base, spread) in spreads.items():
        noise = np.random.default_rng([zlib.crc32(name.encode()), seed]).standard_normal(out[name].shape)
        drawn = base * np.exp(spread * noise) if base else spread * noise
        out[name] = jnp.asarray(drawn.astype(out[name].dtype))
    for name, factor in factors.items():
        out[name] = (out[name] * factor).astype(out[name].dtype)
    return out
```

```python
import numpy as np

import concourse.bass as bass
from concourse import mybir
from concourse.alu_op_type import AluOpType as ALU

ACT = mybir.ActivationFunctionType
F32 = mybir.dt.float32
F32R = mybir.dt.float32r
BF16 = mybir.dt.bfloat16
I32 = mybir.dt.int32
AX_X = mybir.AxisListType.X

P = 128
BANK = 512
TOKENS, HID, HEAD, INTER = 2048, 1024, 256, 2752
PACK, BITS = 8, 4
EPS = 1e-5

CHUNK = 512
CHUNKS = TOKENS // CHUNK
TT = CHUNK // P
KT = HID // P
HT = HEAD // P
NKEY = TOKENS // P
KB = TOKENS // BANK
NH = HID // BANK

HALF = TOKENS // 2
HALVES = TOKENS // HALF
HC = HALF // BANK
HTT = HALF // P
PAIR = 2 * P
PAIRS = -(-INTER // PAIR)
INTER_PAD = PAIRS * PAIR
GROUPS_IN = HID // 128
GROUPS_DOWN = INTER // 128
BLOCKS = PAIRS + 1
ROW_IN = PAIR + PAIR // 2
ROW_DOWN = HID + HID // 2
QUAD = 4
UNIT = QUAD * PAIR
assert UNIT == HID and QUAD * ROW_IN == ROW_DOWN

SBUF_FIRST = 16512


class Map:

    def __init__(self, nc, at):
        self.nc, self.at = nc, at

    def put(self, name, shape, dtype):
        t = self.nc.alloc_sbuf_tensor_at(name, shape, dtype, offset=self.at)
        self.at += -(-int(np.prod(shape[1:])) * (2 if dtype == BF16 else 4) // 32) * 32
        assert self.at <= self.nc.sbuf_usable_end, (name, self.at)
        return t


class Steps:

    def __init__(self, eng, sem, value):
        self.eng, self.sem, self.value = eng, sem, value

    def mark(self, ins):
        ins.then_inc(self.sem, 1)
        self.value = self.value + 1

    def wait(self):
        self.eng.wait_ge(self.sem, self.value)


def wait_apart(eng, keep, sem, value):
    value = value if isinstance(value, int) else eng.to_reg(value)
    eng.wait_ge(keep["const"], 3)
    eng.wait_ge(sem, value)


def three_pass(pe, out, lhs, rhs, first, last):
    pe.matmul(out, lhs[0], rhs[0], start=first, stop=False)
    pe.matmul(out, lhs[0], rhs[1], start=False, stop=False)
    return pe.matmul(out, lhs[1], rhs[0], start=False, stop=last)


def phase_qkv(nc, d, ps, keep, sem):
    m = Map(nc, keep["end"])
    w_f32 = m.put("a_w_f32", [P, KT, 3 * HEAD], F32)
    w_hi = m.put("a_w_hi", [P, KT, 3 * HEAD], F32R)
    w_lo = m.put("a_w_lo", [P, KT, 3 * HEAD], F32R)
    x_f32 = m.put("a_x_f32", [P, KT, CHUNK], F32)
    x_hi = m.put("a_x_hi", [P, KT, CHUNK], F32R)
    x_lo = m.put("a_x_lo", [P, KT, CHUNK], F32R)
    q_hl = m.put("a_q_hl", [P, 2, HT, CHUNK], F32R)
    v_f32 = m.put("a_v_f32", [P, TT, HEAD], F32)
    bias_col = m.put("a_bias_col", [P, 2 * HT], F32)
    bias_v = m.put("a_bias_v", [P, HEAD], F32)
    zp = {"gate": m.put("a_zp_gate", [P, INTER_PAD // PACK], I32), "up": m.put("a_zp_up", [P, INTER_PAD // PACK], I32),
          "down": m.put("a_zp_down", [P, HID // PACK], I32)}
    g_idx = {"gate": m.put("a_g_gate", [P, KT], I32), "up": m.put("a_g_up", [P, KT], I32),
             "down": m.put("a_g_down", [P, 2 * PAIRS], I32)}
    gi_a, gi_b = m.put("a_gi_a", [P, 2 * PAIRS], F32), m.put("a_gi_b", [P, 2 * PAIRS], F32)
    zbf = {"down": m.put("a_zbf_down", [P, HID], BF16)}
    m = Map(nc, keep["end"])
    znib = m.put("a_znib", [P, INTER_PAD // PACK, PACK], I32)
    zbf["gate"] = m.put("a_zbf_gate", [P, INTER_PAD], BF16)
    zbf["up"] = m.put("a_zbf_up", [P, INTER_PAD], BF16)
    assert m.at <= keep["end"] + 4 * KT * 3 * HEAD
    tab_in, tab_out, z_done = sem("a_tab_in"), sem("a_tab_out"), sem("a_z_done")
    k_hi, k_lo, v_hi, v_lo = keep["k_hi"], keep["k_lo"], keep["v_hi"], keep["v_lo"]

    bias_in = sem("a_bias_in")
    w_in = [sem(f"a_w_in{k}") for k in range(KT)]
    x_in = [sem(f"a_x_in{k}") for k in range(KT)]
    q_out = sem("a_q_out")
    whi_done, wlo_done = sem("a_whi_done"), sem("a_wlo_done")
    xhi_done, xlo_done = sem("a_xhi_done"), sem("a_xlo_done")
    x_used = sem("a_x_used")
    qk_ready, v_ready = sem("a_qk_ready"), sem("a_v_ready")
    qkhi_done = sem("a_qkhi_done")
    qklo_done = sem("a_qklo_done")
    v_done = sem("a_v_done")
    vhi_done = sem("a_vhi_done")
    vlo_done = sem("a_vlo_done")

    x_src = d["xT"].rearrange("(k p) t -> k p t", p=P)
    w_src = d["Wqkv"].rearrange("(k p) f -> k p f", p=P)
    q_dst = d["q_scratch"]

    def unpack_zeros(dve, step):
        for n, (name, groups) in enumerate((("gate", GROUPS_IN), ("up", GROUPS_IN), ("down", GROUPS_DOWN))):
            words = zp[name].shape[1]
            if n:
                dve.wait_ge(z_done, n)
            for j in range(PACK):
                ins = dve.tensor_scalar(znib[0:groups, 0:words, j], zp[name][0:groups, :], BITS * j, 15,
                                        ALU.logical_shift_right, ALU.bitwise_and)
            step.mark(ins)
            step.wait()
            dve.tensor_scalar(zbf[name][0:groups, :], znib[0:groups, 0:words, :].rearrange("g w j -> g (w j)"),
                              1.0, None, ALU.add).then_inc(z_done, 1)

    def form_rows(dve, step):
        for name, groups, stride in (("gate", GROUPS_IN, BLOCKS), ("up", GROUPS_IN, BLOCKS), ("down", GROUPS_DOWN, 1)):
            g, out = g_idx[name], keep["row_" + name]
            a, b = gi_a[:, 0:g.shape[1]], gi_b[:, 0:g.shape[1]]
            for make in (lambda: dve.tensor_copy(a, g[:, :]),
                         lambda: dve.tensor_scalar(b, a, 0.0, float(groups), ALU.is_lt, ALU.mult),
                         lambda: dve.tensor_tensor(b, a, b, ALU.add),
                         lambda: dve.tensor_scalar(a, b, 0.0, float(groups - 1), ALU.max, ALU.min),
                         lambda: dve.tensor_scalar(out, a, float(stride), None, ALU.mult)):
                step.mark(make())
                step.wait()

    with nc.Block() as block:
        @block.sync
        def _(sp):
            sp.dma_start(bias_col[:, :], d["bias_qk"]).then_inc(bias_in, 16)
            sp.dma_start(bias_v[:, :], d["bias_v"].to_broadcast([P, HEAD])).then_inc(bias_in, 16)
            for k in range(KT):
                sp.dma_start(w_f32[:, k, :], w_src[k]).then_inc(w_in[k], 16)
                sp.dma_start(x_f32[:, k, :], x_src[k][:, 0:CHUNK]).then_inc(x_in[k], 16)

            def chunk(c, fetch):
                if fetch:
                    for k in range(KT):
                        sp.wait_ge(xlo_done, KT * c + k + 1)
                        sp.dma_start(x_f32[:, k, :], x_src[k][:, bass.ts(c + 1, CHUNK)]).then_inc(x_in[k], 16)
                sp.wait_ge(qklo_done, 4 * c + 4 + 2)
                sp.dma_start(q_dst[c], q_hl[:, :, :, :].rearrange("p s h t -> p (s h t)").bitcast(F32)
                             ).then_inc(q_out, 16)

            with sp.Fori(0, CHUNKS - 1) as c:
                chunk(c, True)
            sp.wait_ge(z_done, 3)
            sp.wait_ge(q_out, 16 * CHUNKS)
            sp.dma_start(keep["q_hl"][:, :, :, :].rearrange("p s h t -> p (s h t)").bitcast(F32), q_dst[0]
                         ).then_inc(keep["q_in"], 16)
            chunk(CHUNKS - 1, False)
            sp.wait_ge(q_out, 16 * (CHUNKS + 1))

        @block.gpsimd
        def _(pool):
            for name, groups in (("gate", GROUPS_IN), ("up", GROUPS_IN), ("down", GROUPS_DOWN)):
                pool.dma_start(zp[name][0:groups, :], d["zeros_" + name]).then_inc(tab_in, 16)
                pool.dma_start(g_idx[name][:, :], d["g_idx_" + name]).then_inc(tab_in, 16)
            for name in ("gate", "up"):
                tab = d["table_" + name].rearrange("(g b) w -> g b w", b=BLOCKS)
                src = d["scales_" + name].rearrange("g (b n) -> g b n", n=PAIR)
                pool.dma_start(tab[:, 0:PAIRS, 0:PAIR], src).then_inc(tab_out, 16)
                pool.dma_start(tab[:, PAIRS:BLOCKS, 0:PAIR], src[:, 0:1, :]).then_inc(tab_out, 16)
            pool.dma_start(d["table_down"][:, 0:HID], d["scales_down"]).then_inc(tab_out, 16)
            pool.memset(keep["ident"][:, :], 0.0).then_inc(keep["const"], 1)
            pool.memset(keep["minus_half"][:, :], -0.5).then_inc(keep["const"], 1)
            pool.wait_ge(keep["const"], 2)
            pool.affine_select(out=keep["ident"][:, :], in_=keep["ident"][:, :], compare_op=ALU.not_equal, fill=1.0,
                               base=0, pattern=[[-1, P]], channel_multiplier=1).then_inc(keep["const"], 1)
            for n, name in enumerate(("gate", "up")):
                pool.wait_ge(z_done, n + 1)
                tab = d["table_" + name].rearrange("(g b) w -> g b w", b=BLOCKS)
                src = zbf[name][0:GROUPS_IN, :].bitcast(F32).rearrange("g (b n) -> g b n", n=PAIR // 2)
                pool.dma_start(tab[:, 0:PAIRS, PAIR:ROW_IN], src).then_inc(tab_out, 16)
                pool.dma_start(tab[:, PAIRS:BLOCKS, PAIR:ROW_IN], src[:, 0:1, :]).then_inc(tab_out, 16)
            pool.wait_ge(z_done, 3)
            pool.dma_start(d["table_down"][:, HID:ROW_DOWN], zbf["down"][0:GROUPS_DOWN, 0:HID].bitcast(F32)
                           ).then_inc(tab_out, 16)
            pool.wait_ge(tab_out, 16 * 10)

        @block.scalar
        def _(act):
            for k in range(KT):
                act.wait_ge(w_in[k], 16)
                act.activation(w_hi[:, k, :], w_f32[:, k, :], ACT.Copy).then_inc(whi_done, 1)
                act.wait_ge(x_in[k], 16)
                act.activation(x_hi[:, k, :], x_f32[:, k, :], ACT.Copy).then_inc(xhi_done, 1)
            act.wait_ge(bias_in, 32)

            def chunk(c, fetch):
                for f in range(4):
                    act.wait_ge(qk_ready, 4 * c + f + 1)
                    if f < HT:
                        act.wait_ge(q_out, 16 * c + 16)
                        out = q_hl[:, 0, f, :]
                    else:
                        out = k_hi[:, f - HT, bass.ts(c, CHUNK)]
                    act.activation(out, ps[:, f, :], ACT.Identity, bias=bias_col[:, f:f + 1]).then_inc(qkhi_done, 1)
                if fetch:
                    for k in range(KT):
                        act.wait_ge(x_in[k], 16 * c + 32)
                        if k < KT - 1:
                            act.wait_ge(x_used, (KT - 1) * c + k + 1)
                        else:
                            act.wait_ge(v_ready, TT * c + TT)
                        act.activation(x_hi[:, k, :], x_f32[:, k, :], ACT.Copy).then_inc(xhi_done, 1)
                for t in range(TT):
                    act.wait_ge(v_done, TT * c + TT + t + 1)
                    act.activation(v_hi[:, bass.ds(c * TT + t, 1), :].rearrange("p a h -> p (a h)"),
                                   v_f32[:, t, :], ACT.Copy).then_inc(vhi_done, 1)

            act.sem_inc(q_out, 16)
            with act.Fori(0, CHUNKS - 1) as c:
                chunk(c, True)
            chunk(CHUNKS - 1, False)

        @block.vector
        def _(dve):
            dve.sem_inc(qklo_done, 4)
            dve.sem_inc(v_done, TT)
            for k in range(KT):
                dve.wait_ge(whi_done, k + 1)
                dve.tensor_tensor(w_lo[:, k, :], w_f32[:, k, :], w_hi[:, k, :].bitcast(F32), ALU.subtract
                                  ).then_inc(wlo_done, 1)
                dve.wait_ge(xhi_done, k + 1)
                dve.tensor_tensor(x_lo[:, k, :], x_f32[:, k, :], x_hi[:, k, :].bitcast(F32), ALU.subtract
                                  ).then_inc(xlo_done, 1)
            dve.wait_ge(tab_in, 16 * 6)
            dve.wait_ge(wlo_done, KT)
            step = Steps(dve, sem("a_step"), 0)
            unpack_zeros(dve, step)
            form_rows(dve, step)
            dve.wait_ge(bias_in, 32)

            def chunk(c, fetch):
                for f in range(4):
                    dve.wait_ge(qkhi_done, 4 * c + f + 1)
                    if f < HT:
                        hi, lo = q_hl[:, 0, f, :], q_hl[:, 1, f, :]
                    else:
                        hi, lo = (t[:, f - HT, bass.ts(c, CHUNK)] for t in (k_hi, k_lo))
                    dve.scalar_tensor_tensor(out=lo, in0=ps[:, f, :], scalar=bias_col[:, f:f + 1], in1=hi.bitcast(F32),
                                             op0=ALU.add, op1=ALU.subtract).then_inc(qklo_done, 1)
                if fetch:
                    for k in range(KT):
                        dve.wait_ge(xhi_done, KT * (c + 1) + k + 1)
                        dve.tensor_tensor(x_lo[:, k, :], x_f32[:, k, :], x_hi[:, k, :].bitcast(F32), ALU.subtract
                                          ).then_inc(xlo_done, 1)
                for t in range(TT):
                    dve.wait_ge(v_ready, TT * c + t + 1)
                    dve.wait_ge(vlo_done, TT * c + t + 1)
                    dve.tensor_tensor(v_f32[:, t, :], ps[:, 4 + t, 0:HEAD], bias_v[:, :], ALU.add).then_inc(v_done, 1)
                for t in range(TT):
                    dve.wait_ge(vhi_done, TT * c + t + 1)
                    tile = bass.ds(c * TT + t, 1)
                    dve.tensor_tensor(v_lo[:, tile, :].rearrange("p a h -> p (a h)"), v_f32[:, t, :],
                                      v_hi[:, tile, :].rearrange("p a h -> p (a h)").bitcast(F32), ALU.subtract
                                      ).then_inc(vlo_done, 1)

            dve.sem_inc(vlo_done, TT)
            with dve.Fori(0, CHUNKS - 1) as c:
                chunk(c, True)
            chunk(CHUNKS - 1, False)

        @block.tensor
        def _(pe):
            with pe.Fori(0, CHUNKS) as c:
                for k in range(KT):
                    pe.wait_ge(wlo_done, k + 1)
                    pe.wait_ge(xlo_done, KT * c + k + 1)
                    for f in range(4):
                        if k == 0:
                            pe.wait_ge(qklo_done, 4 * c + f + 1)
                        col = slice(f * P, (f + 1) * P)
                        mm = three_pass(pe, ps[:, f, :], (w_hi[:, k, col], w_lo[:, k, col]),
                                        (x_hi[:, k, :], x_lo[:, k, :]), k == 0, k == KT - 1)
                        if k == KT - 1:
                            mm.then_inc(qk_ready, 1)
                for k in range(KT):
                    for t in range(TT):
                        if k == 0:
                            pe.wait_ge(v_done, TT * c + t + 1)
                        tok, col = slice(t * P, (t + 1) * P), slice(2 * HEAD, 3 * HEAD)
                        mm = three_pass(pe, ps[:, 4 + t, 0:HEAD], (x_hi[:, k, tok], x_lo[:, k, tok]),
                                        (w_hi[:, k, col], w_lo[:, k, col]), k == 0, k == KT - 1)
                        if k == KT - 1 and t < TT - 1:
                            mm.then_inc(v_ready, 1)
                    mm.then_inc(x_used if k < KT - 1 else v_ready, 1)


def layer_norm_steps(dve, keep, x, stats, mv, step, var_done):
    for h in range(NH):
        ins = dve.bn_stats(stats[:, h, :], x[:, h * BANK:(h + 1) * BANK])
    step.mark(ins)
    wait_apart(dve, keep, step.sem, step.value)
    dve.bn_aggr(mv, stats[:, :, :].rearrange("p h s -> p (h s)")).then_inc(var_done, 1)


def phase_attention(nc, d, ps, keep, sem, feed):
    m = Map(nc, keep["end_q"])
    wo_hi, wo_lo = m.put("b_wo_hi", [P, HT, HID], F32R), m.put("b_wo_lo", [P, HT, HID], F32R)
    bo = m.put("b_bo", [P, HID], F32)
    wo_f32 = Map(nc, m.at).put("b_wo_f32", [P, HT, HID], F32)
    prob = m.put("b_prob", [P, TT, TOKENS], F32)
    RING = 4
    pt_hi, pt_lo = m.put("b_pt_hi", [P, RING, CHUNK], F32R), m.put("b_pt_lo", [P, RING, CHUNK], F32R)
    o_hi, o_lo = m.put("b_o_hi", [P, HT, CHUNK], F32R), m.put("b_o_lo", [P, HT, CHUNK], F32R)
    x = m.put("b_x", [P, TT, HID], F32)
    neg_max, neg_bias = m.put("b_neg_max", [P, TT], F32), m.put("b_neg_bias", [P, TT], F32)
    row_sum, row_inv = m.put("b_row_sum", [P, TT], F32), m.put("b_row_inv", [P, TT], F32)
    stats = m.put("b_stats", [P, NH, 6], F32)
    mv, var_eps, rstd = m.put("b_mv", [P, TT, 2], F32), m.put("b_var_eps", [P, TT], F32), m.put("b_rstd", [P, TT], F32)
    assert m.at <= feed.start
    k_hi, k_lo, v_hi, v_lo = keep["k_hi"], keep["k_lo"], keep["v_hi"], keep["v_lo"]
    q_hl, q_in = keep["q_hl"], keep["q_in"]
    scale = float(HEAD) ** -0.5

    wo_in = sem("b_wo_in")
    x_in = [sem(f"b_x_in{t}") for t in range(TT)]
    x1_out = [sem(f"b_x1_out{t}") for t in range(TT)]
    wohi_done, wolo_done = sem("b_wohi_done"), sem("b_wolo_done")
    scores_ready = sem("b_scores_ready")
    bias_ready, exp_done = sem("b_bias_ready"), sem("b_exp_done")
    pt_ready, pthi_done, ptlo_done, pv_done = (sem(n) for n in ("b_pt_ready", "b_pthi_done", "b_ptlo_done", "b_pv_done"))
    o_ready, ohi_done, olo_done = sem("b_o_ready"), sem("b_ohi_done"), sem("b_olo_done")
    proj_ready = sem("b_proj_ready")
    proj_added = sem("b_proj_added")
    bo_added, var_done, rstd_done, x1_done = (sem(n) for n in ("b_bo_added", "b_var_done", "b_rstd_done", "b_x1_done"))
    step_sem, eps_sem = sem("b_step"), sem("b_eps_step")

    x_tiles = d["x"].rearrange("(n p) h -> n p h", p=P)
    x1_tiles = d["x1_scratch"].rearrange("(n p) h -> n p h", p=P)

    with nc.Block() as block:
        @block.sync
        def _(sp):
            sp.dma_start(wo_f32[:, :, :], d["Wo"].rearrange("(h p) n -> p h n", p=P)).then_inc(wo_in, 16)
            sp.dma_start(bo[:, :], d["bo"].to_broadcast([P, HID])).then_inc(wo_in, 16)
            for t in range(TT):
                sp.sem_inc(x1_out[t], 16)
            sp.dma_start(feed.shift[:, :], d["shift"]).then_inc(feed.shift_in, 16)
            for w in range(2):
                feed.load_in(sp, w, 0)
            for t in range(2):
                feed.load_dn(sp, t, 0)
            with sp.Fori(0, CHUNKS) as c:
                for t in range(TT):
                    sp.wait_ge(x1_out[t], 16 * c + 16)
                    sp.dma_start(x[:, t, :], x_tiles[c * TT + t]).then_inc(x_in[t], 16)
                for t in range(TT):
                    sp.wait_ge(x1_done, TT * c + t + 1)
                    sp.dma_start(x1_tiles[c * TT + t], x[:, t, :]).then_inc(x1_out[t], 16)
            for t in range(2):
                feed.load_ring(sp, 0, t)
            for t in range(TT):
                sp.wait_ge(x1_out[t], 16 * (CHUNKS + 1))

        @block.gpsimd
        def _(pool):
            rows = Steps(pool, feed.row_step, 0)
            feed.first_rows(pool, rows)
            rows.wait()
            for half in range(2):
                feed.gather_in(pool, 0, half)
            pool.wait_ge(wo_in, 32)
            with pool.Fori(0, CHUNKS) as c:
                for t in range(TT):
                    pool.wait_ge(x_in[t], 16 * c + 16)
                    pool.tensor_tensor(out=x[:, t, :], in0=x[:, t, :], in1=bo[:, :], op=ALU.add).then_inc(bo_added, 1)
                for t in range(TT):
                    wait_apart(pool, keep, var_done, TT * c + t + 1)
                    pool.tensor_scalar(var_eps[:, t:t + 1], mv[:, t, 1:2], EPS, None, ALU.add).then_inc(eps_sem, 1)
                    pool.wait_ge(eps_sem, TT * c + t + 1)
                    pool.tensor_tensor(out=rstd[:, t:t + 1], in0=var_eps[:, t:t + 1], in1=keep["minus_half"][:, 0:1],
                                       op=ALU.pow).then_inc(rstd_done, 1)

        @block.scalar
        def _(act):
            act.wait_ge(wo_in, 32)
            for h in range(HT):
                act.activation(wo_hi[:, h, :], wo_f32[:, h, :], ACT.Copy).then_inc(wohi_done, 1)

            def chunk(c, fetch):
                for t in range(TT):
                    act.wait_ge(bias_ready, TT * c + t + 1)
                    bank = KB * (t % 2)
                    act.activation(prob[:, t, :], ps[:, bank:bank + KB, :].rearrange("p b n -> p (b n)"), ACT.Exp,
                                   bias=neg_bias[:, t:t + 1], scale=scale, accum_out=row_sum[:, t:t + 1]
                                   ).then_inc(exp_done, 1)
                if fetch:
                    act.wait_ge(scores_ready, TT * c + TT)
                    act.dma_start(q_hl[:, :, :, :].rearrange("p s h t -> p (s h t)").bitcast(F32),
                                  d["q_scratch"][c + 1]).then_inc(q_in, 16)
                for k in range(NKEY):
                    act.wait_ge(pt_ready, NKEY * c + k + 1)
                    if k >= RING:
                        act.wait_ge(pv_done, (NKEY - 1) * c + k - RING + 1)
                    act.activation(pt_hi[:, k % RING, :], ps[:, k % 2, :], ACT.Copy).then_inc(pthi_done, 1)
                for h in range(HT):
                    act.wait_ge(o_ready, c + 1)
                    act.activation(o_hi[:, h, :], ps[:, 2 + h, :], ACT.Copy).then_inc(ohi_done, 1)

            with act.Fori(0, CHUNKS - 1) as c:
                chunk(c, True)
            chunk(CHUNKS - 1, False)

        @block.vector
        def _(dve):
            dve.sem_inc(proj_added, TT)
            for h in range(HT):
                dve.wait_ge(wohi_done, h + 1)
                dve.tensor_tensor(wo_lo[:, h, :], wo_f32[:, h, :], wo_hi[:, h, :].bitcast(F32), ALU.subtract
                                  ).then_inc(wolo_done, 1)
            STEPS = 2 * TT + 1

            def chunk(c, last):
                step = Steps(dve, step_sem, STEPS * c)
                for t in range(TT):
                    dve.wait_ge(scores_ready, TT * c + t + 1)
                    bank = KB * (t % 2)
                    step.mark(dve.tensor_reduce(neg_max[:, t:t + 1], ps[:, bank:bank + KB, :].rearrange("p b n -> p (b n)"),
                                                AX_X, ALU.max, negate=True))
                    step.wait()
                    dve.tensor_scalar(neg_bias[:, t:t + 1], neg_max[:, t:t + 1], scale, None, ALU.mult
                                      ).then_inc(bias_ready, 1)
                for k in range(NKEY):
                    dve.wait_ge(pthi_done, NKEY * c + k + 1)
                    dve.tensor_tensor(pt_lo[:, k % RING, :], ps[:, k % 2, :], pt_hi[:, k % RING, :].bitcast(F32),
                                      ALU.subtract).then_inc(ptlo_done, 1)
                for h in range(HT):
                    dve.wait_ge(ohi_done, HT * c + h + 1)
                    dve.tensor_tensor(o_lo[:, h, :], ps[:, 2 + h, :], o_hi[:, h, :].bitcast(F32), ALU.subtract
                                      ).then_inc(olo_done, 1)
                if last:
                    dve.wait_ge(feed.shift_in, 16)
                    for half in range(2):
                        feed.unpack(dve, half, half, 16 * QUAD, 0, 0)
                step.mark(dve.reciprocal(row_inv[:, :], row_sum[:, :]))
                step.wait()

                def normalise(t):
                    dve.wait_ge(rstd_done, TT * c + t + 1)
                    dve.tensor_scalar(x[:, t, :], x[:, t, :], mv[:, t, 0:1], rstd[:, t:t + 1], ALU.subtract, ALU.mult
                                      ).then_inc(x1_done, 1)

                for t in range(TT):
                    dve.wait_ge(proj_ready, TT * c + t + 1)
                    dve.wait_ge(bo_added, TT * c + t + 1)
                    bank = 4 + NH * (t % 2)
                    dve.scalar_tensor_tensor(out=x[:, t, :], in0=ps[:, bank:bank + NH, :].rearrange("p b n -> p (b n)"),
                                             scalar=row_inv[:, t:t + 1], in1=x[:, t, :], op0=ALU.mult, op1=ALU.add
                                             ).then_inc(proj_added, 1)
                    dve.wait_ge(proj_added, TT * c + TT + t + 1)
                    layer_norm_steps(dve, keep, x[:, t, :], stats, mv[:, t, :], step, var_done)
                    if t:
                        normalise(t - 1)
                normalise(TT - 1)

            with dve.Fori(0, CHUNKS - 1) as c:
                chunk(c, False)
            chunk(CHUNKS - 1, True)

        @block.tensor
        def _(pe):
            pe.wait_ge(keep["const"], 3)
            with pe.Fori(0, CHUNKS) as c:
                pe.wait_ge(q_in, 16 * c + 16)
                for t in range(TT):
                    if t == 1:
                        pe.wait_ge(proj_added, TT * c + TT)
                    if t >= 2:
                        pe.wait_ge(exp_done, TT * c + t - 1)
                    for b in range(KB):
                        for h in range(HT):
                            lhs = [q_hl[:, s, h, t * P:(t + 1) * P] for s in range(2)]
                            rhs = [k[:, h, b * BANK:(b + 1) * BANK] for k in (k_hi, k_lo)]
                            mm = three_pass(pe, ps[:, KB * (t % 2) + b, :], lhs, rhs, h == 0, h == HT - 1)
                    mm.then_inc(scores_ready, 1)

                def turn(k):
                    if k == 0:
                        pe.wait_ge(exp_done, TT * c + TT)
                    if k >= 2:
                        pe.wait_ge(ptlo_done, NKEY * c + k - 1)
                    for t in range(TT):
                        tr = pe.transpose(ps[:, k % 2, t * P:(t + 1) * P], prob[:, t, k * P:(k + 1) * P],
                                          keep["ident"][:, :])
                    tr.then_inc(pt_ready, 1)

                turn(0)
                turn(1)
                for k in range(NKEY):
                    pe.wait_ge(ptlo_done, NKEY * c + k + 1)
                    for h in range(HT):
                        lhs = [v[:, k, h * P:(h + 1) * P] for v in (v_hi, v_lo)]
                        rhs = [pt[:, k % RING, :] for pt in (pt_hi, pt_lo)]
                        mm = three_pass(pe, ps[:, 2 + h, :], lhs, rhs, k == 0, k == NKEY - 1)
                    mm.then_inc(pv_done if k < NKEY - 1 else o_ready, 1)
                    if k + 2 < NKEY:
                        turn(k + 2)
                pe.wait_ge(wolo_done, HT)
                pe.wait_ge(olo_done, HT * c + HT)
                for t in range(TT):
                    if t >= 2:
                        pe.wait_ge(proj_added, TT * c + TT + t - 1)
                    for n in range(NH):
                        for h in range(HT):
                            lhs = [o[:, h, t * P:(t + 1) * P] for o in (o_hi, o_lo)]
                            rhs = [w[:, h, n * BANK:(n + 1) * BANK] for w in (wo_hi, wo_lo)]
                            mm = three_pass(pe, ps[:, 4 + NH * (t % 2) + n, :], lhs, rhs, h == 0, h == HT - 1)
                    mm.then_inc(proj_ready, 1)


DN0, DN1, GA, GB, UA, UB = range(6)
UNITS = 6
PRO = 4


def unit(g, u):
    return g * UNITS + (PRO + u)


class Feed:

    def __init__(self, nc, d, keep, sem):
        self.d, self.keep = d, keep
        words = ROW_DOWN * 2 + UNIT * 2 + PAIR * 2 + HID * 2 + 2 * HC * BANK + 2 * KT + 8 + 8
        self.start = (nc.sbuf_usable_end - 4 * words) // 32 * 32 - 32
        m = Map(nc, self.start)
        self.sz = m.put("f_sz", [P, 2, ROW_DOWN], F32)
        self.wt = m.put("f_wt", [P, 2, UNIT], F32)
        self.q_in = m.put("f_q_in", [P, 2, PAIR], I32)
        self.q_dn = m.put("f_q_dn", [P, 2, HID], I32)
        self.silu = m.put("f_silu", [P, 2 * HC, BANK], F32)
        self.x_ring = self.silu[:, :, :].rearrange("p (s n) t -> p s (n t)", s=2)
        self.cur_in = m.put("f_cur_in", [P, 2, KT], I32)
        self.cur_dn = m.put("f_cur_dn", [P, 2], I32)
        self.shift = m.put("f_shift", [P, 1], I32)
        self.shift_in = sem("f_shift_in")
        self.qin_in = [sem(f"f_qin_in{w}") for w in range(2)]
        self.qdn_in = [sem(f"f_qdn_in{t}") for t in range(2)]
        self.sz_in = [sem(f"f_sz_in{s}") for s in range(2)]
        self.ring_in = [sem(f"f_ring_in{s}") for s in range(2)]
        self.row_step, self.unit_step = sem("f_row_step"), sem("f_unit_step")
        self.w_made, self.wlo_done = sem("f_w_made"), sem("f_wlo_done")
        self.qdn_src = d["q_down"].rearrange("(t r) n -> t r n", r=P // PACK)
        self.x1_tiles = d["x1_scratch"].rearrange("(h n p) c -> h n p c", h=HALVES, p=P)

    def load_in(self, sp, w, blk):
        sp.dma_start(self.q_in[:, w, :], self.d[("q_gate", "q_up")[w]][blk]).then_inc(self.qin_in[w], 16)

    def load_dn(self, sp, t, blk):
        src = self.qdn_src[2 * blk + t].unsqueeze(1).to_broadcast([P // PACK, PACK, HID])
        sp.dma_start(self.q_dn[:, t, :], src).then_inc(self.qdn_in[t], 16)

    def load_ring(self, sp, h, t):
        sp.dma_start(self.x_ring[:, t % 2, :], self.x1_tiles[h, t]).then_inc(self.ring_in[t % 2], 16)

    def first_rows(self, pool, step):
        for w, name in enumerate(("gate", "up")):
            ins = pool.tensor_copy(self.cur_in[:, w, :], self.keep["row_" + name])
        step.mark(ins)

    def gather(self, pool, slot, part, table, rows, width):
        pool.indirect_dma_start(out=self.sz[:, slot, part * width:(part + 1) * width], out_offset=None, in_=table,
                                in_offset=bass.IndirectOffsetOnAxis(ap=rows, axis=0)).then_inc(self.sz_in[slot], 16)

    def gather_in(self, pool, w, half):
        for i in range(QUAD):
            rows = self.cur_in[:, w, QUAD * half + i:QUAD * half + i + 1]
            self.gather(pool, half, i, self.d[("table_gate", "table_up")[w]], rows, ROW_IN)

    def gather_dn(self, pool, t):
        self.gather(pool, t, 0, self.d["table_down"], self.cur_dn[:, t:t + 1], ROW_DOWN)

    def unpack(self, dve, n, slot, landed, w, g):
        step = Steps(dve, self.unit_step, n * 2)
        val, sz = self.wt[:, slot, :], self.sz[:, slot, :]
        if not (isinstance(n, int) and n < 2):
            dve.wait_ge(self.wlo_done, n - 1)
        if w is None:
            dve.wait_ge(self.qdn_in[slot], g * 16 + 16)
            ins = dve.tensor_scalar(val.bitcast(I32), self.q_dn[:, slot, :], self.shift[:, 0:1], 15,
                                    ALU.logical_shift_right, ALU.bitwise_and)
            ints, scale, zero = val.bitcast(I32), sz[:, 0:HID], sz.bitcast(BF16)[:, 2 * HID:3 * HID]
        else:
            dve.wait_ge(self.qin_in[w], g * 16 + 16)
            for i in range(QUAD):
                ins = dve.tensor_scalar(val.bitcast(I32)[:, i * PAIR:(i + 1) * PAIR], self.q_in[:, w, :],
                                        BITS * (QUAD * slot + i), 15, ALU.logical_shift_right, ALU.bitwise_and)
            ints = val.bitcast(I32).rearrange("p (i n) -> p i n", i=QUAD)
            val = val.rearrange("p (i n) -> p i n", i=QUAD)
            scale = sz.rearrange("p (i w) -> p i w", i=QUAD)[:, :, 0:PAIR]
            zero = sz.bitcast(BF16).rearrange("p (i w) -> p i w", i=QUAD)[:, :, 2 * PAIR:3 * PAIR]
        step.mark(ins)
        step.wait()
        dve.wait_ge(self.sz_in[slot], landed)
        step.mark(dve.tensor_tensor(val, ints, zero, ALU.subtract))
        step.wait()
        dve.tensor_tensor(val, val, scale, ALU.mult).then_inc(self.w_made, 1)


def phase_mlp(nc, d, ps, keep, sem, feed):
    m = Map(nc, keep["end_const"])
    x_hi, x_lo = m.put("c_x_hi", [P, KT, HALF], F32R), m.put("c_x_lo", [P, KT, HALF], F32R)
    acc = m.put("c_acc", [P, HTT, HID], F32)
    in_hi, in_lo = m.put("c_in_hi", [P, 2, KT, PAIR], F32R), m.put("c_in_lo", [P, 2, KT, PAIR], F32R)
    dn_hi, dn_lo = m.put("c_dn_hi", [P, 2, HID], F32R), m.put("c_dn_lo", [P, 2, HID], F32R)
    h_hi, h_lo = m.put("c_h_hi", [P, 2, HALF], F32R), m.put("c_h_lo", [P, 2, HALF], F32R)
    h_f32 = m.put("c_h_f32", [P, 2, BANK], F32)
    stats = m.put("c_stats", [P, HTT, NH, 6], F32)
    mv, var_eps, rstd = m.put("c_mv", [P, HTT, 2], F32), m.put("c_var_eps", [P, HTT], F32), m.put("c_rstd", [P, HTT], F32)
    neg_mean = m.put("c_neg_mean", [P, HTT], F32)

    assert m.at <= feed.start
    silu, x_ring, wt = feed.silu, feed.x_ring, feed.wt
    ring_in, sz_in, row_step, unit_step, w_made, wlo_done = (
        feed.ring_in, feed.sz_in, feed.row_step, feed.unit_step, feed.w_made, feed.wlo_done)
    acc_in = [sem(f"c_acc_in{t}") for t in range(HTT)]
    out_done = [sem(f"c_out_done{t}") for t in range(HTT)]
    ln_step, eps_step, whi_done = sem("c_ln_step"), sem("c_eps_step"), sem("c_whi_done")
    xt_ready, xhi_done, xlo_done = sem("c_xt_ready"), sem("c_xhi_done"), sem("c_xlo_done")
    gate_ready, up_ready = sem("c_gate_ready"), sem("c_up_ready")
    down_ready = sem("c_down_ready")
    silu_done, h_made, hhi_done, hlo_done = sem("c_silu_done"), sem("c_h_made"), sem("c_hhi_done"), sem("c_hlo_done")
    acc_done = sem("c_acc_done")
    var_done, rstd_done, x2_done = sem("c_var_done"), sem("c_rstd_done"), sem("c_x2_done")

    BLK = 2 * HC
    DN = HTT * NH
    XT = HTT * 2
    assert BLK == 4 and DN == 16

    x1_tiles = d["x1_scratch"].rearrange("(h n p) c -> h n p c", h=HALVES, p=P)
    out_tiles = d["out"].rearrange("(h n p) c -> h n p c", h=HALVES, p=P)

    def halves(eng, body):
        for h in range(HALVES):
            with eng.Fori(0, PAIRS - 1) as p:
                body(h, p, p + h * PAIRS, False)
            body(h, PAIRS - 1, h * PAIRS + PAIRS - 1, True)
            yield h

    def more(h, last):
        return not (last and h == HALVES - 1)

    with nc.Block() as block:
        @block.sync
        def _(sp):
            def body(h, p, g, last):
                if more(h, last):
                    for t in range(2):
                        sp.wait_ge(unit_step, unit(g, DN0 + t) * 2 + 1)
                        feed.load_dn(sp, t, p + 1)
                    sp.wait_ge(unit_step, unit(g, GB) * 2 + 1)
                    feed.load_in(sp, 0, p + 2)
                    if last:
                        sp.wait_ge(h_made, g * BLK + 2 * BLK)
                        for t in range(HTT):
                            if t >= 2:
                                sp.wait_ge(xt_ready, XT * (h + 1) + 2 * (t - 2) + 2)
                            feed.load_ring(sp, h + 1, t)
                    sp.wait_ge(unit_step, unit(g, UB) * 2 + 1)
                    feed.load_in(sp, 1, p + 2)

            for t in range(2, HTT):
                sp.wait_ge(xt_ready, 2 * (t - 2) + 2)
                feed.load_ring(sp, 0, t)
            sp.wait_ge(unit_step, 2 * 1 + 1)
            feed.load_in(sp, 0, 1)
            sp.wait_ge(unit_step, 2 * 3 + 1)
            feed.load_in(sp, 1, 1)
            for t in range(HTT):
                sp.dma_start(acc[:, t, :], x1_tiles[0, t]).then_inc(acc_in[t], 16)
            for h in halves(sp, body):
                for t in range(HTT):
                    sp.wait_ge(x2_done, HTT * h + t + 1)
                    sp.dma_start(out_tiles[h, t], acc[:, t, :]).then_inc(out_done[t], 16)
                for t in range(HTT):
                    sp.wait_ge(out_done[t], 16 * (h + 1))
                    if h < HALVES - 1:
                        sp.dma_start(acc[:, t, :], x1_tiles[h + 1, t]).then_inc(acc_in[t], 16)

        @block.gpsimd
        def _(pool):
            def body(h, p, g, last):
                step = Steps(pool, row_step, g * 2 + (h + 1))
                for s in range(2):
                    pool.wait_ge(sz_in[s], g * (16 + 128) + 128)
                step.mark(pool.tensor_copy(feed.cur_dn[:, :], keep["row_down"][:, bass.ts(p, 2)]))
                step.mark(pool.tensor_scalar(feed.cur_in[:, :, :], feed.cur_in[:, :, :], 1.0, None, ALU.add))
                step.wait()
                for t in range(2):
                    wait_apart(pool, keep, w_made, unit(g, DN0 + t) - 1)
                    feed.gather_dn(pool, t)
                if more(h, last):
                    for w in range(2):
                        for half in range(2):
                            wait_apart(pool, keep, w_made, unit(g, GA + 2 * w + half) - 1)
                            feed.gather_in(pool, w, half)

            for half in range(2):
                pool.wait_ge(w_made, 2 + half - 1)
                feed.gather_in(pool, 1, half)
            for h in halves(pool, body):
                if h < HALVES - 1:
                    for s in range(2):
                        pool.wait_ge(sz_in[s], (h + 1) * PAIRS * (16 + 128) + 128)
                    feed.first_rows(pool, Steps(pool, row_step, 2 * PAIRS * (h + 1) + h + 1))
                step = Steps(pool, eps_step, 3 * HTT * h)
                for t in range(HTT):
                    pool.wait_ge(var_done, HTT * h + t + 1)
                    step.mark(pool.tensor_scalar(var_eps[:, t:t + 1], mv[:, t, 1:2], EPS, None, ALU.add))
                    step.mark(pool.tensor_scalar(neg_mean[:, t:t + 1], mv[:, t, 0:1], -1.0, None, ALU.mult))
                    step.wait()
                    step.mark(pool.tensor_tensor(out=rstd[:, t:t + 1], in0=var_eps[:, t:t + 1],
                                                 in1=keep["minus_half"][:, 0:1], op=ALU.pow))
                    step.wait()
                    pool.tensor_tensor(out=neg_mean[:, t:t + 1], in0=neg_mean[:, t:t + 1], in1=rstd[:, t:t + 1],
                                       op=ALU.mult).then_inc(rstd_done, 1)

        @block.scalar
        def _(act):
            def in_hi_unit(n, w, half):
                out = in_hi[:, w, QUAD * half:QUAD * (half + 1), :].rearrange("p i n -> p (i n)")
                act.wait_ge(w_made, n + 1)
                act.activation(out, wt[:, half, :], ACT.Copy).then_inc(whi_done, 1)

            def x_hi_quad(h, k, bank):
                act.wait_ge(xt_ready, XT * h + k + 1)
                t, quad = k // 2, k % 2
                act.activation(x_hi[:, QUAD * quad:QUAD * (quad + 1), t * P:(t + 1) * P],
                               ps[:, bank, :].rearrange("p (i t) -> p i t", t=P), ACT.Copy).then_inc(xhi_done, 1)

            def body(h, p, g, last):
                for b in range(BLK):
                    act.wait_ge(gate_ready, g * BLK + b + 1)
                    if b == 0:
                        act.wait_ge(h_made, g * BLK + BLK)
                    act.activation(silu[:, b, :], ps[:, b, :], ACT.Silu).then_inc(silu_done, 1)
                    if b < 2:
                        act.wait_ge(w_made, unit(g, DN0 + b) + 1)
                        act.wait_ge(down_ready, g * DN + DN)
                        act.activation(dn_hi[:, b, :], wt[:, b, :], ACT.Copy).then_inc(whi_done, 1)

                def h_high(b):
                    act.wait_ge(h_made, g * BLK + BLK + b + 1)
                    act.activation(h_hi[:, b // HC, (b % HC) * BANK:(b % HC + 1) * BANK], h_f32[:, b % 2, :], ACT.Copy
                                   ).then_inc(hhi_done, 1)

                if more(h, last):
                    act.wait_ge(gate_ready, g * BLK + BLK)
                    in_hi_unit(unit(g, GA), 0, 0)
                h_high(0)
                if more(h, last):
                    in_hi_unit(unit(g, GB), 0, 1)
                for b in range(1, BLK):
                    h_high(b)
                turned = last and h < HALVES - 1
                if last:
                    for t in range(HTT + 1):
                        if turned and t < HTT:
                            for k in (2 * t, 2 * t + 1):
                                x_hi_quad(h + 1, k, x_bank(k))
                        if t:
                            act.wait_ge(rstd_done, HTT * h + t)
                            act.activation(acc[:, t - 1, :], acc[:, t - 1, :], ACT.Identity, scale=rstd[:, t - 1:t],
                                           bias=neg_mean[:, t - 1:t]).then_inc(x2_done, 1)
                if more(h, last):
                    act.wait_ge(up_ready, g * BLK + BLK)
                    in_hi_unit(unit(g, UA), 1, 0)
                    in_hi_unit(unit(g, UB), 1, 1)

            act.sem_inc(h_made, BLK)
            in_hi_unit(0, 0, 0)
            in_hi_unit(1, 0, 1)
            for k in range(XT):
                x_hi_quad(0, k, x0_bank(k))
            in_hi_unit(2, 1, 0)
            in_hi_unit(3, 1, 1)
            for h in halves(act, body):
                pass

        @block.vector
        def _(dve):
            def w_low(n, slot, hi, lo):
                dve.wait_ge(whi_done, n + 1)
                dve.tensor_tensor(lo, wt[:, slot, :], hi.bitcast(F32), ALU.subtract).then_inc(wlo_done, 1)

            def in_low(n, w, half):
                hi, lo = (t[:, w, QUAD * half:QUAD * (half + 1), :].rearrange("p i n -> p (i n)") for t in (in_hi, in_lo))
                w_low(n, half, hi, lo)

            def x_low_quad(h, k, bank):
                dve.wait_ge(xhi_done, XT * h + k + 1)
                t, quad = k // 2, k % 2
                hi, lo = (x[:, QUAD * quad:QUAD * (quad + 1), t * P:(t + 1) * P] for x in (x_hi, x_lo))
                dve.tensor_tensor(lo, ps[:, bank, :].rearrange("p (i t) -> p i t", t=P), hi.bitcast(F32), ALU.subtract
                                  ).then_inc(xlo_done, 1)

            def body(h, p, g, last):
                turned = last and h < HALVES - 1
                step = Steps(dve, ln_step, HTT * h)

                def h_make(b):
                    dve.wait_ge(up_ready, g * BLK + b + 1)
                    dve.wait_ge(silu_done, g * BLK + b + 1)
                    if b >= 2:
                        dve.wait_ge(hlo_done, g * BLK + b - 1)
                    dve.tensor_tensor(h_f32[:, b % 2, :], silu[:, b, :], ps[:, 4 + b, :], ALU.mult).then_inc(h_made, 1)

                def h_low(b):
                    dve.wait_ge(hhi_done, g * BLK + b + 1)
                    hi, lo = (t[:, b // HC, (b % HC) * BANK:(b % HC + 1) * BANK] for t in (h_hi, h_lo))
                    dve.tensor_tensor(lo, h_f32[:, b % 2, :], hi.bitcast(F32), ALU.subtract).then_inc(hlo_done, 1)

                def add(n):
                    t, b = n // NH, n % NH
                    part = acc[:, t, b * BANK:(b + 1) * BANK]
                    dve.wait_ge(down_ready, g * DN + DN + n + 1)
                    if b == 0:
                        dve.wait_ge(acc_in[t], 16 * (h + 1))
                    bank = (4 * t + b) % 8 if turned else n % 8
                    dve.tensor_tensor(part, ps[:, bank, :], part, ALU.add).then_inc(acc_done, 1)

                def add_tile(t):
                    for n in range(NH * t, NH * t + NH):
                        add(n)
                    if turned:
                        for k in (2 * t, 2 * t + 1):
                            x_low_quad(h + 1, k, x_bank(k))
                    if last:
                        dve.wait_ge(acc_done, g * DN + DN + NH * (t + 1))
                        layer_norm_steps(dve, keep, acc[:, t, :], stats[:, t, :, :], mv[:, t, :], step, var_done)

                landed = g * (16 + 128) + 128
                feed.unpack(dve, unit(g, DN0), 0, landed + 16, None, g)
                feed.unpack(dve, unit(g, DN1), 1, landed + 16, None, g)
                w_low(unit(g, DN0), 0, dn_hi[:, 0, :], dn_lo[:, 0, :])
                w_low(unit(g, DN1), 1, dn_hi[:, 1, :], dn_lo[:, 1, :])
                if more(h, last):
                    feed.unpack(dve, unit(g, GA), 0, landed + 80, 0, g + 1)
                h_make(0)
                if more(h, last):
                    in_low(unit(g, GA), 0, 0)
                    feed.unpack(dve, unit(g, GB), 1, landed + 80, 0, g + 1)
                h_make(1)
                h_low(0)
                if more(h, last):
                    in_low(unit(g, GB), 0, 1)
                h_low(1)
                h_make(2)
                h_low(2)
                h_make(3)
                h_low(3)
                if more(h, last):
                    if turned:
                        for t in range(HTT):
                            add_tile(t)
                    feed.unpack(dve, unit(g, UA), 0, landed + 144, 1, g + 1)
                    if not turned:
                        add_tile(0)
                        add_tile(1)
                    in_low(unit(g, UA), 1, 0)
                    feed.unpack(dve, unit(g, UB), 1, landed + 144, 1, g + 1)
                    if not turned:
                        add_tile(2)
                        add_tile(3)
                    in_low(unit(g, UB), 1, 1)
                    for t in range(4, 0 if turned else HTT):
                        add_tile(t)
                else:
                    for t in range(HTT):
                        add_tile(t)

            dve.sem_inc(acc_done, DN)
            in_low(0, 0, 0)
            in_low(1, 0, 1)
            for k in range(XT):
                x_low_quad(0, k, x0_bank(k))
            feed.unpack(dve, 2, 0, 128, 1, 0)
            in_low(2, 1, 0)
            feed.unpack(dve, 3, 1, 128, 1, 0)
            in_low(3, 1, 1)
            for h in halves(dve, body):
                pass

        @block.tensor
        def _(pe):
            def turn(h, k, bank):
                t, quad = k // 2, k % 2
                if quad == 0:
                    pe.wait_ge(ring_in[t % 2], 16 * (HTT // 2 * h + t // 2 + 1))
                cols = x_ring[:, t % 2, :].rearrange("p (r i) -> p i r", i=PACK)
                for i in range(QUAD):
                    tr = pe.transpose(ps[:, bank, i * P:(i + 1) * P], cols[:, QUAD * quad + i, :], keep["ident"][:, :])
                tr.then_inc(xt_ready, 1)

            def body(h, p, g, last):
                turned = last and h < HALVES - 1
                for w, ready in ((0, gate_ready), (1, up_ready)):
                    for j in range(2):
                        for c in range(HC):
                            b = HC * j + c
                            pe.wait_ge(acc_done, g * DN + 8 + 4 * w + b + 1)
                            for i in range(KT):
                                if i == 0 and b < HC and w == 0:
                                    pe.wait_ge(xlo_done, XT * h + 2 * TT * (c + 1))
                                if b == 0 and i % QUAD == 0:
                                    pe.wait_ge(wlo_done, g * UNITS + 2 * w + i // QUAD + 1)
                                cols, toks = slice(j * P, (j + 1) * P), slice(c * BANK, (c + 1) * BANK)
                                mm = three_pass(pe, ps[:, 4 * w + b, :], (in_hi[:, w, i, cols], in_lo[:, w, i, cols]),
                                                (x_hi[:, i, toks], x_lo[:, i, toks]), i == 0, i == KT - 1)
                            mm.then_inc(ready, 1)
                pe.wait_ge(wlo_done, unit(g, DN1) + 1)
                for t in range(HTT):
                    if t % TT == 0:
                        pe.wait_ge(hlo_done, g * BLK + HC + t // TT + 1)
                    for b in range(NH):
                        n, e = NH * t + b, 4 * t + b if turned else NH * t + b
                        bank = e % 8
                        if e < 4:
                            pe.wait_ge(silu_done, g * BLK + bank + 1)
                        elif e < 8:
                            pe.wait_ge(h_made, g * BLK + BLK + bank - 4 + 1)
                        else:
                            pe.wait_ge(acc_done, g * DN + DN + (n - 4 if turned else n - 8) + 1)
                        for j in range(2):
                            toks, cols = slice(t * P, (t + 1) * P), slice(b * BANK, (b + 1) * BANK)
                            mm = three_pass(pe, ps[:, bank, :], (h_hi[:, j, toks], h_lo[:, j, toks]),
                                            (dn_hi[:, j, cols], dn_lo[:, j, cols]), j == 0, j == 1)
                        mm.then_inc(down_ready, 1)
                    if turned:
                        for k in (2 * t, 2 * t + 1):
                            if t == 0:
                                pe.wait_ge(silu_done, g * BLK + x_bank(k) + 1)
                            elif t == 1:
                                pe.wait_ge(h_made, g * BLK + BLK + x_bank(k) - 4 + 1)
                            else:
                                pe.wait_ge(xlo_done, XT * (h + 1) + k - 4 + 1)
                            turn(h + 1, k, x_bank(k))

            pe.sem_inc(down_ready, DN)
            for k in range(XT):
                if k >= 8:
                    pe.wait_ge(xlo_done, k - 4 + 1)
                turn(0, k, x0_bank(k))
            for h in halves(pe, body):
                if h < HALVES - 1:
                    pe.wait_ge(acc_done, DN * PAIRS * (h + 1) + DN)


def x0_bank(k):
    return k if k < 8 else 4 + k % 4


def x_bank(k):
    return (4 * (k // 2) + 2 + k % 2) % 8


def build(nc, d, out):
    d["out"] = out
    sems = {}

    def sem(name):
        sems[name] = nc.alloc_semaphore(name)
        return sems[name]

    d["q_scratch"] = nc.dram_tensor("q_scratch", (CHUNKS, P, 2 * HT * CHUNK), F32).ap()
    d["x1_scratch"] = nc.dram_tensor("x1_scratch", (TOKENS, HID), F32).ap()
    d["table_gate"] = nc.dram_tensor("table_gate", (GROUPS_IN * BLOCKS, ROW_IN), F32).ap()
    d["table_up"] = nc.dram_tensor("table_up", (GROUPS_IN * BLOCKS, ROW_IN), F32).ap()
    d["table_down"] = nc.dram_tensor("table_down", (GROUPS_DOWN, ROW_DOWN), F32).ap()

    m = Map(nc, SBUF_FIRST)
    ident, minus_half = m.put("ident", [P, P], F32), m.put("minus_half", [P, 1], F32)
    keep = {"ident": ident, "minus_half": minus_half, "const": sem("const")}
    for name, n in (("gate", KT), ("up", KT), ("down", 2 * PAIRS)):
        keep["row_" + name] = m.put("row_" + name, [P, n], I32)[:, :]
    keep["end_const"] = m.at
    for name in ("k_hi", "k_lo"):
        keep[name] = m.put(name, [P, HT, TOKENS], F32R)
    for name in ("v_hi", "v_lo"):
        keep[name] = m.put(name, [P, NKEY, HEAD], F32R)
    keep["end"] = m.at
    keep["q_hl"] = m.put("b_q_hl", [P, 2, HT, CHUNK], F32R)
    keep["q_in"], keep["end_q"] = sem("b_q_in"), m.at
    with nc.psum_tensor("ps", [P, 8, BANK], F32) as ps:
        phase_qkv(nc, d, ps, keep, sem)
        feed = Feed(nc, d, keep, sem)
        phase_attention(nc, d, ps, keep, sem, feed)
        phase_mlp(nc, d, ps, keep, sem, feed)


def _blocks(a, wrap):
    out = np.zeros((P, PAIRS, PAIR), a.dtype)
    out.reshape(P, INTER_PAD)[:, :INTER] = a
    out = out.transpose(1, 0, 2)
    return np.ascontiguousarray(np.concatenate([out, out[:wrap]]))


def _wide(a, n, axis):
    shape = list(a.shape)
    shape[axis] = n
    out = np.zeros(shape, a.dtype)
    out[tuple(slice(0, s) for s in a.shape)] = a
    return out


def kernel(**inputs):
    import concourse.bacc as bacc
    from concourse.bass_utils import run_bass_kernel_spmd

    a = {k.removeprefix("L0_"): np.asarray(v) for k, v in inputs.items()}
    x = a["attn_x"].reshape(TOKENS, HID)
    q_down = _wide(a["ffn_down_qweight"], (PAIRS + 1) * PAIR // PACK, 0)
    q_down[PAIRS * PAIR // PACK:] = q_down[:PAIR // PACK]
    arrays = {
        "x": x,
        "xT": np.ascontiguousarray(x.T),
        "Wqkv": a["attn_Wqkv"],
        "bias_qk": np.ascontiguousarray(a["attn_bqkv"][:2 * HEAD].reshape(2 * HT, P).T),
        "bias_v": a["attn_bqkv"][2 * HEAD:].reshape(1, HEAD),
        "Wo": a["attn_Wo"],
        "bo": a["attn_bo"].reshape(1, HID),
        "q_gate": _blocks(a["ffn_gate_qweight"], 2),
        "q_up": _blocks(a["ffn_up_qweight"], 2),
        "q_down": q_down,
        "scales_gate": _wide(a["ffn_gate_scales"], INTER_PAD, 1),
        "scales_up": _wide(a["ffn_up_scales"], INTER_PAD, 1),
        "scales_down": a["ffn_down_scales"],
        "zeros_gate": _wide(a["ffn_gate_qzeros"], INTER_PAD // PACK, 1),
        "zeros_up": _wide(a["ffn_up_qzeros"], INTER_PAD // PACK, 1),
        "zeros_down": a["ffn_down_qzeros"],
        "g_idx_gate": a["ffn_gate_g_idx"].reshape(P, KT),
        "g_idx_up": a["ffn_up_g_idx"].reshape(P, KT),
        "g_idx_down": np.ascontiguousarray(_wide(a["ffn_down_g_idx"], INTER_PAD, 0).reshape(2 * PAIRS, P).T),
        "shift": np.tile(np.arange(0, 32, BITS, dtype=np.int32), P // PACK).reshape(P, 1),
    }
    arrays = {k: np.ascontiguousarray(v) for k, v in arrays.items()}

    nc = bacc.Bacc("TRN2", target_bir_lowering=False, num_devices=1)
    d = {k: nc.dram_tensor(k, v.shape, mybir.dt.from_np(v.dtype), kind="ExternalInput").ap() for k, v in arrays.items()}
    out = nc.dram_tensor("out", (TOKENS, HID), F32, kind="ExternalOutput").ap()
    build(nc, d, out)
    r = run_bass_kernel_spmd(nc, [arrays], core_ids=[0])
    return r.results[0]["out"].reshape(1, TOKENS, HID)
```

```python
import numpy as np

import concourse.bass as bass
from concourse import mybir
from concourse.alu_op_type import AluOpType as ALU

ACT = mybir.ActivationFunctionType
F32 = mybir.dt.float32
F32R = mybir.dt.float32r
BF16 = mybir.dt.bfloat16
I32 = mybir.dt.int32
AX_X = mybir.AxisListType.X

P = 128
BANK = 512
TOKENS, HID, HEAD, INTER = 2048, 1024, 256, 2752
PACK, BITS = 8, 4
EPS = 1e-5

CHUNK = 512
CHUNKS = TOKENS // CHUNK
TT = CHUNK // P
KT = HID // P
HT = HEAD // P
NKEY = TOKENS // P
KB = TOKENS // BANK
NH = HID // BANK

HALF = TOKENS // 2
HALVES = TOKENS // HALF
HC = HALF // BANK
HTT = HALF // P
PAIR = 2 * P
PAIRS = -(-INTER // PAIR)
INTER_PAD = PAIRS * PAIR
GROUPS_IN = HID // 128
GROUPS_DOWN = INTER // 128
BLOCKS = PAIRS + 1
ROW_IN = PAIR + PAIR // 2
ROW_DOWN = HID + HID // 2
QUAD = 4
UNIT = QUAD * PAIR
assert UNIT == HID and QUAD * ROW_IN == ROW_DOWN

SBUF_FIRST = 16512


class Map:

    def __init__(self, nc, at):
        self.nc, self.at = nc, at

    def put(self, name, shape, dtype):
        t = self.nc.alloc_sbuf_tensor_at(name, shape, dtype, offset=self.at)
        self.at += -(-int(np.prod(shape[1:])) * (2 if dtype == BF16 else 4) // 32) * 32
        assert self.at <= self.nc.sbuf_usable_end, (name, self.at)
        return t


class Steps:

    def __init__(self, eng, sem, value):
        self.eng, self.sem, self.value = eng, sem, value

    def mark(self, ins):
        ins.then_inc(self.sem, 1)
        self.value = self.value + 1

    def wait(self):
        self.eng.wait_ge(self.sem, self.value)


def wait_apart(eng, keep, sem, value):
    value = value if isinstance(value, int) else eng.to_reg(value)
    eng.wait_ge(keep["const"], 3)
    eng.wait_ge(sem, value)


def three_pass(pe, out, lhs, rhs, first, last):
    pe.matmul(out, lhs[0], rhs[0], start=first, stop=False)
    pe.matmul(out, lhs[0], rhs[1], start=False, stop=False)
    return pe.matmul(out, lhs[1], rhs[0], start=False, stop=last)


def phase_qkv(nc, d, ps, keep, sem):
    m = Map(nc, keep["end"])
    w_f32 = m.put("a_w_f32", [P, KT, 3 * HEAD], F32)
    w_hi = m.put("a_w_hi", [P, KT, 3 * HEAD], F32R)
    w_lo = m.put("a_w_lo", [P, KT, 3 * HEAD], F32R)
    x_f32 = m.put("a_x_f32", [P, KT, CHUNK], F32)
    x_hi = m.put("a_x_hi", [P, KT, CHUNK], F32R)
    x_lo = m.put("a_x_lo", [P, KT, CHUNK], F32R)
    q_hl = m.put("a_q_hl", [P, 2, HT, CHUNK], F32R)
    v_f32 = m.put("a_v_f32", [P, TT, HEAD], F32)
    bias_col = m.put("a_bias_col", [P, 2 * HT], F32)
    bias_v = m.put("a_bias_v", [P, HEAD], F32)
    zp = {"gate": m.put("a_zp_gate", [P, INTER_PAD // PACK], I32), "up": m.put("a_zp_up", [P, INTER_PAD // PACK], I32),
          "down": m.put("a_zp_down", [P, HID // PACK], I32)}
    g_idx = {"gate": m.put("a_g_gate", [P, KT], I32), "up": m.put("a_g_up", [P, KT], I32),
             "down": m.put("a_g_down", [P, 2 * PAIRS], I32)}
    gi_a, gi_b = m.put("a_gi_a", [P, 2 * PAIRS], F32), m.put("a_gi_b", [P, 2 * PAIRS], F32)
    zbf = {"down": m.put("a_zbf_down", [P, HID], BF16)}
    m = Map(nc, keep["end"])
    znib = m.put("a_znib", [P, INTER_PAD // PACK, PACK], I32)
    zbf["gate"] = m.put("a_zbf_gate", [P, INTER_PAD], BF16)
    zbf["up"] = m.put("a_zbf_up", [P, INTER_PAD], BF16)
    assert m.at <= keep["end"] + 4 * KT * 3 * HEAD
    tab_in, tab_out, z_done = sem("a_tab_in"), sem("a_tab_out"), sem("a_z_done")
    k_hi, k_lo, v_hi, v_lo = keep["k_hi"], keep["k_lo"], keep["v_hi"], keep["v_lo"]

    bias_in = sem("a_bias_in")
    w_in = [sem(f"a_w_in{k}") for k in range(KT)]
    x_in = [sem(f"a_x_in{k}") for k in range(KT)]
    q_out = sem("a_q_out")
    whi_done, wlo_done = sem("a_whi_done"), sem("a_wlo_done")
    xhi_done, xlo_done = sem("a_xhi_done"), sem("a_xlo_done")
    x_used = sem("a_x_used")
    qk_ready, v_ready = sem("a_qk_ready"), sem("a_v_ready")
    qkhi_done = sem("a_qkhi_done")
    qklo_done = sem("a_qklo_done")
    v_done = sem("a_v_done")
    vhi_done = sem("a_vhi_done")
    vlo_done = sem("a_vlo_done")

    x_src = d["xT"].rearrange("(k p) t -> k p t", p=P)
    w_src = d["Wqkv"].rearrange("(k p) f -> k p f", p=P)
    q_dst = d["q_scratch"]

    def unpack_zeros(dve, step):
        for n, (name, groups) in enumerate((("gate", GROUPS_IN), ("up", GROUPS_IN), ("down", GROUPS_DOWN))):
            words = zp[name].shape[1]
            if n:
                dve.wait_ge(z_done, n)
            for j in range(PACK):
                ins = dve.tensor_scalar(znib[0:groups, 0:words, j], zp[name][0:groups, :], BITS * j, 15,
                                        ALU.logical_shift_right, ALU.bitwise_and)
            step.mark(ins)
            step.wait()
            dve.tensor_scalar(zbf[name][0:groups, :], znib[0:groups, 0:words, :].rearrange("g w j -> g (w j)"),
                              1.0, None, ALU.add).then_inc(z_done, 1)

    def form_rows(dve, step):
        for name, groups, stride in (("gate", GROUPS_IN, BLOCKS), ("up", GROUPS_IN, BLOCKS), ("down", GROUPS_DOWN, 1)):
            g, out = g_idx[name], keep["row_" + name]
            a, b = gi_a[:, 0:g.shape[1]], gi_b[:, 0:g.shape[1]]
            for make in (lambda: dve.tensor_copy(a, g[:, :]),
                         lambda: dve.tensor_scalar(b, a, 0.0, float(groups), ALU.is_lt, ALU.mult),
                         lambda: dve.tensor_tensor(b, a, b, ALU.add),
                         lambda: dve.tensor_scalar(a, b, 0.0, float(groups - 1), ALU.max, ALU.min),
                         lambda: dve.tensor_scalar(out, a, float(stride), None, ALU.mult)):
                step.mark(make())
                step.wait()

    with nc.Block() as block:
        @block.sync
        def _(sp):
            sp.dma_start(bias_col[:, :], d["bias_qk"]).then_inc(bias_in, 16)
            sp.dma_start(bias_v[:, :], d["bias_v"].to_broadcast([P, HEAD])).then_inc(bias_in, 16)
            for k in range(KT):
                sp.dma_start(w_f32[:, k, :], w_src[k]).then_inc(w_in[k], 16)
                sp.dma_start(x_f32[:, k, :], x_src[k][:, 0:CHUNK]).then_inc(x_in[k], 16)

            def chunk(c, fetch):
                if fetch:
                    for k in range(KT):
                        sp.wait_ge(xlo_done, KT * c + k + 1)
                        sp.dma_start(x_f32[:, k, :], x_src[k][:, bass.ts(c + 1, CHUNK)]).then_inc(x_in[k], 16)
                sp.wait_ge(qklo_done, 4 * c + 4 + 2)
                sp.dma_start(q_dst[c], q_hl[:, :, :, :].rearrange("p s h t -> p (s h t)").bitcast(F32)
                             ).then_inc(q_out, 16)

            with sp.Fori(0, CHUNKS - 1) as c:
                chunk(c, True)
            sp.wait_ge(z_done, 3)
            sp.wait_ge(q_out, 16 * CHUNKS)
            sp.dma_start(keep["q_hl"][:, :, :, :].rearrange("p s h t -> p (s h t)").bitcast(F32), q_dst[0]
                         ).then_inc(keep["q_in"], 16)
            chunk(CHUNKS - 1, False)
            sp.wait_ge(q_out, 16 * (CHUNKS + 1))

        @block.gpsimd
        def _(pool):
            for name, groups in (("gate", GROUPS_IN), ("up", GROUPS_IN), ("down", GROUPS_DOWN)):
                pool.dma_start(zp[name][0:groups, :], d["zeros_" + name]).then_inc(tab_in, 16)
                pool.dma_start(g_idx[name][:, :], d["g_idx_" + name]).then_inc(tab_in, 16)
            for name in ("gate", "up"):
                tab = d["table_" + name].rearrange("(g b) w -> g b w", b=BLOCKS)
                src = d["scales_" + name].rearrange("g (b n) -> g b n", n=PAIR)
                pool.dma_start(tab[:, 0:PAIRS, 0:PAIR], src).then_inc(tab_out, 16)
                pool.dma_start(tab[:, PAIRS:BLOCKS, 0:PAIR], src[:, 0:1, :]).then_inc(tab_out, 16)
            pool.dma_start(d["table_down"][:, 0:HID], d["scales_down"]).then_inc(tab_out, 16)
            pool.memset(keep["ident"][:, :], 0.0).then_inc(keep["const"], 1)
            pool.memset(keep["minus_half"][:, :], -0.5).then_inc(keep["const"], 1)
            pool.wait_ge(keep["const"], 2)
            pool.affine_select(out=keep["ident"][:, :], in_=keep["ident"][:, :], compare_op=ALU.not_equal, fill=1.0,
                               base=0, pattern=[[-1, P]], channel_multiplier=1).then_inc(keep["const"], 1)
            for n, name in enumerate(("gate", "up")):
                pool.wait_ge(z_done, n + 1)
                tab = d["table_" + name].rearrange("(g b) w -> g b w", b=BLOCKS)
                src = zbf[name][0:GROUPS_IN, :].bitcast(F32).rearrange("g (b n) -> g b n", n=PAIR // 2)
                pool.dma_start(tab[:, 0:PAIRS, PAIR:ROW_IN], src).then_inc(tab_out, 16)
                pool.dma_start(tab[:, PAIRS:BLOCKS, PAIR:ROW_IN], src[:, 0:1, :]).then_inc(tab_out, 16)
            pool.wait_ge(z_done, 3)
            pool.dma_start(d["table_down"][:, HID:ROW_DOWN], zbf["down"][0:GROUPS_DOWN, 0:HID].bitcast(F32)
                           ).then_inc(tab_out, 16)
            pool.wait_ge(tab_out, 16 * 10)

        @block.scalar
        def _(act):
            for k in range(KT):
                act.wait_ge(w_in[k], 16)
                act.activation(w_hi[:, k, :], w_f32[:, k, :], ACT.Copy).then_inc(whi_done, 1)
                act.wait_ge(x_in[k], 16)
                act.activation(x_hi[:, k, :], x_f32[:, k, :], ACT.Copy).then_inc(xhi_done, 1)
            act.wait_ge(bias_in, 32)

            def chunk(c, fetch):
                for f in range(4):
                    act.wait_ge(qk_ready, 4 * c + f + 1)
                    if f < HT:
                        act.wait_ge(q_out, 16 * c + 16)
                        out = q_hl[:, 0, f, :]
                    else:
                        out = k_hi[:, f - HT, bass.ts(c, CHUNK)]
                    act.activation(out, ps[:, f, :], ACT.Identity, bias=bias_col[:, f:f + 1]).then_inc(qkhi_done, 1)
                if fetch:
                    for k in range(KT):
                        act.wait_ge(x_in[k], 16 * c + 32)
                        if k < KT - 1:
                            act.wait_ge(x_used, (KT - 1) * c + k + 1)
                        else:
                            act.wait_ge(v_ready, TT * c + TT)
                        act.activation(x_hi[:, k, :], x_f32[:, k, :], ACT.Copy).then_inc(xhi_done, 1)
                for t in range(TT):
                    act.wait_ge(v_done, TT * c + TT + t + 1)
                    act.activation(v_hi[:, bass.ds(c * TT + t, 1), :].rearrange("p a h -> p (a h)"),
                                   v_f32[:, t, :], ACT.Copy).then_inc(vhi_done, 1)

            act.sem_inc(q_out, 16)
            with act.Fori(0, CHUNKS - 1) as c:
                chunk(c, True)
            chunk(CHUNKS - 1, False)

        @block.vector
        def _(dve):
            dve.sem_inc(qklo_done, 4)
            dve.sem_inc(v_done, TT)
            for k in range(KT):
                dve.wait_ge(whi_done, k + 1)
                dve.tensor_tensor(w_lo[:, k, :], w_f32[:, k, :], w_hi[:, k, :].bitcast(F32), ALU.subtract
                                  ).then_inc(wlo_done, 1)
                dve.wait_ge(xhi_done, k + 1)
                dve.tensor_tensor(x_lo[:, k, :], x_f32[:, k, :], x_hi[:, k, :].bitcast(F32), ALU.subtract
                                  ).then_inc(xlo_done, 1)
            dve.wait_ge(tab_in, 16 * 6)
            dve.wait_ge(wlo_done, KT)
            step = Steps(dve, sem("a_step"), 0)
            unpack_zeros(dve, step)
            form_rows(dve, step)
            dve.wait_ge(bias_in, 32)

            def chunk(c, fetch):
                for f in range(4):
                    dve.wait_ge(qkhi_done, 4 * c + f + 1)
                    if f < HT:
                        hi, lo = q_hl[:, 0, f, :], q_hl[:, 1, f, :]
                    else:
                        hi, lo = (t[:, f - HT, bass.ts(c, CHUNK)] for t in (k_hi, k_lo))
                    dve.scalar_tensor_tensor(out=lo, in0=ps[:, f, :], scalar=bias_col[:, f:f + 1], in1=hi.bitcast(F32),
                                             op0=ALU.add, op1=ALU.subtract).then_inc(qklo_done, 1)
                if fetch:
                    for k in range(KT):
                        dve.wait_ge(xhi_done, KT * (c + 1) + k + 1)
                        dve.tensor_tensor(x_lo[:, k, :], x_f32[:, k, :], x_hi[:, k, :].bitcast(F32), ALU.subtract
                                          ).then_inc(xlo_done, 1)
                for t in range(TT):
                    dve.wait_ge(v_ready, TT * c + t + 1)
                    dve.wait_ge(vlo_done, TT * c + t + 1)
                    dve.tensor_tensor(v_f32[:, t, :], ps[:, 4 + t, 0:HEAD], bias_v[:, :], ALU.add).then_inc(v_done, 1)
                for t in range(TT):
                    dve.wait_ge(vhi_done, TT * c + t + 1)
                    tile = bass.ds(c * TT + t, 1)
                    dve.tensor_tensor(v_lo[:, tile, :].rearrange("p a h -> p (a h)"), v_f32[:, t, :],
                                      v_hi[:, tile, :].rearrange("p a h -> p (a h)").bitcast(F32), ALU.subtract
                                      ).then_inc(vlo_done, 1)

            dve.sem_inc(vlo_done, TT)
            with dve.Fori(0, CHUNKS - 1) as c:
                chunk(c, True)
            chunk(CHUNKS - 1, False)

        @block.tensor
        def _(pe):
            with pe.Fori(0, CHUNKS) as c:
                for k in range(KT):
                    pe.wait_ge(wlo_done, k + 1)
                    pe.wait_ge(xlo_done, KT * c + k + 1)
                    for f in range(4):
                        if k == 0:
                            pe.wait_ge(qklo_done, 4 * c + f + 1)
                        col = slice(f * P, (f + 1) * P)
                        mm = three_pass(pe, ps[:, f, :], (w_hi[:, k, col], w_lo[:, k, col]),
                                        (x_hi[:, k, :], x_lo[:, k, :]), k == 0, k == KT - 1)
                        if k == KT - 1:
                            mm.then_inc(qk_ready, 1)
                for k in range(KT):
                    for t in range(TT):
                        if k == 0:
                            pe.wait_ge(v_done, TT * c + t + 1)
                        tok, col = slice(t * P, (t + 1) * P), slice(2 * HEAD, 3 * HEAD)
                        mm = three_pass(pe, ps[:, 4 + t, 0:HEAD], (x_hi[:, k, tok], x_lo[:, k, tok]),
                                        (w_hi[:, k, col], w_lo[:, k, col]), k == 0, k == KT - 1)
                        if k == KT - 1 and t < TT - 1:
                            mm.then_inc(v_ready, 1)
                    mm.then_inc(x_used if k < KT - 1 else v_ready, 1)


def layer_norm_steps(dve, keep, x, stats, mv, step, var_done):
    for h in range(NH):
        ins = dve.bn_stats(stats[:, h, :], x[:, h * BANK:(h + 1) * BANK])
    step.mark(ins)
    wait_apart(dve, keep, step.sem, step.value)
    dve.bn_aggr(mv, stats[:, :, :].rearrange("p h s -> p (h s)")).then_inc(var_done, 1)


def phase_attention(nc, d, ps, keep, sem, feed):
    m = Map(nc, keep["end_q"])
    wo_hi, wo_lo = m.put("b_wo_hi", [P, HT, HID], F32R), m.put("b_wo_lo", [P, HT, HID], F32R)
    bo = m.put("b_bo", [P, HID], F32)
    wo_f32 = Map(nc, m.at).put("b_wo_f32", [P, HT, HID], F32)
    prob = m.put("b_prob", [P, TT, TOKENS], F32)
    RING = 4
    pt_hi, pt_lo = m.put("b_pt_hi", [P, RING, CHUNK], F32R), m.put("b_pt_lo", [P, RING, CHUNK], F32R)
    x = m.put("b_x", [P, TT, HID], F32)
    o_hi, o_lo = m.put("b_o_hi", [P, HT, CHUNK], F32R), m.put("b_o_lo", [P, HT, CHUNK], F32R)
    neg_max, neg_bias = m.put("b_neg_max", [P, TT], F32), m.put("b_neg_bias", [P, TT], F32)
    row_sum, row_inv = m.put("b_row_sum", [P, TT], F32), m.put("b_row_inv", [P, TT], F32)
    stats = m.put("b_stats", [P, NH, 6], F32)
    mv, var_eps, rstd = m.put("b_mv", [P, TT, 2], F32), m.put("b_var_eps", [P, TT], F32), m.put("b_rstd", [P, TT], F32)
    assert m.at <= feed.start_b
    k_hi, k_lo, v_hi, v_lo = keep["k_hi"], keep["k_lo"], keep["v_hi"], keep["v_lo"]
    q_hl, q_in = keep["q_hl"], keep["q_in"]
    scale = float(HEAD) ** -0.5

    wo_in = sem("b_wo_in")
    x_in = [sem(f"b_x_in{t}") for t in range(TT)]
    x1_out = feed.x1_out
    wohi_done, wolo_done = sem("b_wohi_done"), sem("b_wolo_done")
    scores_ready = sem("b_scores_ready")
    bias_ready, exp_done = sem("b_bias_ready"), sem("b_exp_done")
    pt_ready, pthi_done, ptlo_done, pv_done = (sem(n) for n in ("b_pt_ready", "b_pthi_done", "b_ptlo_done", "b_pv_done"))
    o_ready, ohi_done, olo_done = sem("b_o_ready"), sem("b_ohi_done"), sem("b_olo_done")
    proj_ready = sem("b_proj_ready")
    proj_added = sem("b_proj_added")
    bo_added, var_done, rstd_done, x1_done = (sem(n) for n in ("b_bo_added", "b_var_done", "b_rstd_done", "b_x1_done"))
    step_sem, eps_sem = sem("b_step"), sem("b_eps_step")

    x_tiles = d["x"].rearrange("(n p) h -> n p h", p=P)
    x1_tiles = d["x1_scratch"].rearrange("(n p) h -> n p h", p=P)

    with nc.Block() as block:
        @block.sync
        def _(sp):
            sp.dma_start(wo_f32[:, :, :], d["Wo"].rearrange("(h p) n -> p h n", p=P)).then_inc(wo_in, 16)
            sp.dma_start(bo[:, :], d["bo"].to_broadcast([P, HID])).then_inc(wo_in, 16)
            for t in range(TT):
                sp.sem_inc(x1_out[t], 16)
            sp.dma_start(feed.shift[:, :], d["shift"]).then_inc(feed.shift_in, 16)
            for w in range(2):
                feed.load_in(sp, w, 0)
            for t in range(2):
                feed.load_dn(sp, t, 0)

            def chunk(c):
                for t in range(TT):
                    sp.wait_ge(x1_out[t], 16 * c + 16)
                    sp.dma_start(x[:, t, :], x_tiles[c * TT + t]).then_inc(x_in[t], 16)
                for t in range(TT):
                    sp.wait_ge(x1_done, TT * c + t + 1)
                    sp.dma_start(x1_tiles[c * TT + t], x[:, t, :]).then_inc(x1_out[t], 16)

            with sp.Fori(0, CHUNKS - 1) as c:
                chunk(c)
            for t in range(2):
                feed.load_ring(sp, 0, t)
            chunk(CHUNKS - 1)

        @block.gpsimd
        def _(pool):
            rows = Steps(pool, feed.row_step, 0)
            feed.first_rows(pool, rows)
            rows.wait()
            for u in (GA, GB):
                feed.gather(pool, u)
            pool.wait_ge(wo_in, 32)
            with pool.Fori(0, CHUNKS) as c:
                for t in range(TT):
                    pool.wait_ge(x_in[t], 16 * c + 16)
                    pool.tensor_tensor(out=x[:, t, :], in0=x[:, t, :], in1=bo[:, :], op=ALU.add).then_inc(bo_added, 1)
                for t in range(TT):
                    wait_apart(pool, keep, var_done, TT * c + t + 1)
                    pool.tensor_scalar(var_eps[:, t:t + 1], mv[:, t, 1:2], EPS, None, ALU.add).then_inc(eps_sem, 1)
                    pool.wait_ge(eps_sem, TT * c + t + 1)
                    pool.tensor_tensor(out=rstd[:, t:t + 1], in0=var_eps[:, t:t + 1], in1=keep["minus_half"][:, 0:1],
                                       op=ALU.pow).then_inc(rstd_done, 1)

        @block.scalar
        def _(act):
            act.wait_ge(wo_in, 32)
            for h in range(HT):
                act.activation(wo_hi[:, h, :], wo_f32[:, h, :], ACT.Copy).then_inc(wohi_done, 1)

            def chunk(c, fetch):
                for t in range(TT):
                    act.wait_ge(bias_ready, TT * c + t + 1)
                    bank = KB * (t % 2)
                    act.activation(prob[:, t, :], ps[:, bank:bank + KB, :].rearrange("p b n -> p (b n)"), ACT.Exp,
                                   bias=neg_bias[:, t:t + 1], scale=scale, accum_out=row_sum[:, t:t + 1]
                                   ).then_inc(exp_done, 1)
                if fetch:
                    act.wait_ge(scores_ready, TT * c + TT)
                    act.dma_start(q_hl[:, :, :, :].rearrange("p s h t -> p (s h t)").bitcast(F32),
                                  d["q_scratch"][c + 1]).then_inc(q_in, 16)
                for k in range(NKEY):
                    act.wait_ge(pt_ready, NKEY * c + k + 1)
                    if k >= RING:
                        act.wait_ge(pv_done, (NKEY - 1) * c + k - RING + 1)
                    act.activation(pt_hi[:, k % RING, :], ps[:, k % 2, :], ACT.Copy).then_inc(pthi_done, 1)
                for h in range(HT):
                    act.wait_ge(o_ready, c + 1)
                    act.activation(o_hi[:, h, :], ps[:, 2 + h, :], ACT.Copy).then_inc(ohi_done, 1)

            with act.Fori(0, CHUNKS - 1) as c:
                chunk(c, True)
            chunk(CHUNKS - 1, False)

        @block.vector
        def _(dve):
            dve.sem_inc(proj_added, TT)
            for h in range(HT):
                dve.wait_ge(wohi_done, h + 1)
                dve.tensor_tensor(wo_lo[:, h, :], wo_f32[:, h, :], wo_hi[:, h, :].bitcast(F32), ALU.subtract
                                  ).then_inc(wolo_done, 1)

            def low(c, k):
                dve.wait_ge(pthi_done, NKEY * c + k + 1)
                dve.tensor_tensor(pt_lo[:, k % RING, :], ps[:, k % 2, :], pt_hi[:, k % RING, :].bitcast(F32),
                                  ALU.subtract).then_inc(ptlo_done, 1)

            def add(j, t):
                dve.wait_ge(proj_ready, TT * j + t + 1)
                dve.wait_ge(bo_added, TT * j + t + 1)
                dve.scalar_tensor_tensor(out=x[:, t, :], in0=ps[:, NH * t:NH * t + NH, :].rearrange("p b n -> p (b n)"),
                                         scalar=row_inv[:, t:t + 1], in1=x[:, t, :], op0=ALU.mult, op1=ALU.add
                                         ).then_inc(proj_added, 1)

            def statistics(j, t, step):
                dve.wait_ge(proj_added, TT * j + TT + t + 1)
                layer_norm_steps(dve, keep, x[:, t, :], stats, mv[:, t, :], step, var_done)

            def normalise(j, t):
                dve.wait_ge(rstd_done, TT * j + t + 1)
                dve.tensor_scalar(x[:, t, :], x[:, t, :], mv[:, t, 0:1], rstd[:, t:t + 1], ALU.subtract, ALU.mult
                                  ).then_inc(x1_done, 1)

            def chunk(c, step):
                first = isinstance(c, int)
                for t in range(TT):
                    dve.wait_ge(scores_ready, TT * c + t + 1)
                    bank = KB * (t % 2)
                    step.mark(dve.tensor_reduce(neg_max[:, t:t + 1], ps[:, bank:bank + KB, :].rearrange("p b n -> p (b n)"),
                                                AX_X, ALU.max, negate=True))
                    step.wait()
                    dve.tensor_scalar(neg_bias[:, t:t + 1], neg_max[:, t:t + 1], scale, None, ALU.mult
                                      ).then_inc(bias_ready, 1)
                if not first:
                    for t in range(TT - 1):
                        add(c - 1, t)
                        statistics(c - 1, t, step)
                        if t:
                            normalise(c - 1, t - 1)
                    add(c - 1, TT - 1)
                low(c, 0)
                low(c, 1)
                if not first:
                    statistics(c - 1, TT - 1, step)
                low(c, 2)
                if not first:
                    normalise(c - 1, TT - 2)
                low(c, 3)
                if not first:
                    normalise(c - 1, TT - 1)
                for k in range(4, NKEY):
                    low(c, k)
                for h in range(HT):
                    dve.wait_ge(ohi_done, HT * c + h + 1)
                    dve.tensor_tensor(o_lo[:, h, :], ps[:, 2 + h, :], o_hi[:, h, :].bitcast(F32), ALU.subtract
                                      ).then_inc(olo_done, 1)
                step.mark(dve.reciprocal(row_inv[:, :], row_sum[:, :]))
                step.wait()

            chunk(0, Steps(dve, step_sem, 0))
            FIRST, STEPS = TT + 1, 2 * TT + 1
            with dve.Fori(0, CHUNKS - 1) as i:
                chunk(i + 1, Steps(dve, step_sem, STEPS * i + FIRST))
            dve.wait_ge(feed.shift_in, 16)
            for u in (GA, GB):
                feed.unpack(dve, -1, u)
            step = Steps(dve, step_sem, STEPS * (CHUNKS - 1) + FIRST)
            for t in range(TT):
                add(CHUNKS - 1, t)
                statistics(CHUNKS - 1, t, step)
                if t:
                    normalise(CHUNKS - 1, t - 1)
            normalise(CHUNKS - 1, TT - 1)

        @block.tensor
        def _(pe):
            def project(j, t):
                for n in range(NH):
                    for h in range(HT):
                        lhs = [o[:, h, t * P:(t + 1) * P] for o in (o_hi, o_lo)]
                        rhs = [w[:, h, n * BANK:(n + 1) * BANK] for w in (wo_hi, wo_lo)]
                        mm = three_pass(pe, ps[:, NH * t + n, :], lhs, rhs, h == 0, h == HT - 1)
                mm.then_inc(proj_ready, 1)

            def chunk(c):
                first = isinstance(c, int)
                pe.wait_ge(q_in, 16 * c + 16)
                if not first:
                    pe.wait_ge(ptlo_done, NKEY * c)
                    pe.wait_ge(olo_done, HT * c)
                for t in range(TT):
                    if t == 1 and not first:
                        pe.wait_ge(proj_added, TT * c)
                    if t >= 2:
                        pe.wait_ge(exp_done, TT * c + t - 1)
                    for b in range(KB):
                        for h in range(HT):
                            lhs = [q_hl[:, s, h, t * P:(t + 1) * P] for s in range(2)]
                            rhs = [k[:, h, b * BANK:(b + 1) * BANK] for k in (k_hi, k_lo)]
                            mm = three_pass(pe, ps[:, KB * (t % 2) + b, :], lhs, rhs, h == 0, h == HT - 1)
                    mm.then_inc(scores_ready, 1)
                if not first:
                    for t in range(TT):
                        pe.wait_ge(exp_done, TT * c + 3 + t // 2)
                        project(c - 1, t)

                def turn(k):
                    if k == 0:
                        pe.wait_ge(exp_done, TT * c + TT)
                        if not first:
                            pe.wait_ge(proj_added, TT * c + 2)
                    if k >= 2:
                        pe.wait_ge(ptlo_done, NKEY * c + k - 1)
                    for t in range(TT):
                        tr = pe.transpose(ps[:, k % 2, t * P:(t + 1) * P], prob[:, t, k * P:(k + 1) * P],
                                          keep["ident"][:, :])
                    tr.then_inc(pt_ready, 1)

                turn(0)
                turn(1)
                for k in range(NKEY):
                    pe.wait_ge(ptlo_done, NKEY * c + k + 1)
                    for h in range(HT):
                        lhs = [v[:, k, h * P:(h + 1) * P] for v in (v_hi, v_lo)]
                        rhs = [pt[:, k % RING, :] for pt in (pt_hi, pt_lo)]
                        mm = three_pass(pe, ps[:, 2 + h, :], lhs, rhs, k == 0, k == NKEY - 1)
                    mm.then_inc(pv_done if k < NKEY - 1 else o_ready, 1)
                    if k + 2 < NKEY:
                        turn(k + 2)

            pe.wait_ge(keep["const"], 3)
            chunk(0)
            pe.wait_ge(wolo_done, HT)
            with pe.Fori(0, CHUNKS - 1) as i:
                chunk(i + 1)
            pe.wait_ge(olo_done, HT * CHUNKS)
            for t in range(TT):
                if t == 2:
                    pe.wait_ge(proj_added, TT * CHUNKS)
                project(CHUNKS - 1, t)


DN0, DN1, GA, GB, UA, UB = range(6)
UNITS = 6
GATES = {GA: (0, 0), GB: (0, 1), UA: (1, 0), UB: (1, 1)}
SZ_SLOT = (1, 2, 0, 1, 2, 0)
SZ_FIRST, SZ_PAIR = (128, 64, 64), (128, 80, 80)
SZ_WITH = (16, 16, 64, 80, 80, 128)
PRO = 4


def unit(g, u):
    return g * UNITS + (PRO + u)


class Feed:

    def __init__(self, nc, d, keep, sem):
        self.d, self.keep = d, keep
        words = ROW_DOWN * 3 + UNIT * 2 + PAIR * 2 + HID * 2 + 2 * HC * BANK + 2 * KT + 8 + 8
        self.start = (nc.sbuf_usable_end - 4 * words) // 32 * 32 - 32
        m = Map(nc, self.start)
        sz2 = m.put("f_sz2", [P, ROW_DOWN], F32)
        self.start_b = m.at
        sz = m.put("f_sz", [P, 2, ROW_DOWN], F32)
        self.sz = [sz[:, 0, :], sz[:, 1, :], sz2[:, :]]
        self.wt = m.put("f_wt", [P, 2, UNIT], F32)
        self.q_in = m.put("f_q_in", [P, 2, PAIR], I32)
        self.q_dn = m.put("f_q_dn", [P, 2, HID], I32)
        self.silu = m.put("f_silu", [P, 2 * HC, BANK], F32)
        self.x_ring = self.silu[:, :, :].rearrange("p (s n) t -> p s (n t)", s=2)
        self.cur_in = m.put("f_cur_in", [P, 2, KT], I32)
        self.cur_dn = m.put("f_cur_dn", [P, 2], I32)
        self.shift = m.put("f_shift", [P, 1], I32)
        self.shift_in = sem("f_shift_in")
        self.qin_in = [sem(f"f_qin_in{w}") for w in range(2)]
        self.qdn_in = [sem(f"f_qdn_in{t}") for t in range(2)]
        self.sz_in = [sem(f"f_sz_in{s}") for s in range(3)]
        self.ring_in = [sem(f"f_ring_in{s}") for s in range(2)]
        self.x1_out = [sem(f"b_x1_out{t}") for t in range(TT)]
        self.row_step, self.unit_step = sem("f_row_step"), sem("f_unit_step")
        self.w_made, self.wlo_done = sem("f_w_made"), sem("f_wlo_done")
        self.qdn_src = d["q_down"].rearrange("(t r) n -> t r n", r=P // PACK)
        self.x1_tiles = d["x1_scratch"].rearrange("(h n p) c -> h n p c", h=HALVES, p=P)

    def load_in(self, sp, w, blk):
        sp.dma_start(self.q_in[:, w, :], self.d[("q_gate", "q_up")[w]][blk]).then_inc(self.qin_in[w], 16)

    def load_dn(self, sp, t, blk):
        src = self.qdn_src[2 * blk + t].unsqueeze(1).to_broadcast([P // PACK, PACK, HID])
        sp.dma_start(self.q_dn[:, t, :], src).then_inc(self.qdn_in[t], 16)

    def load_ring(self, sp, h, t):
        sp.dma_start(self.x_ring[:, t % 2, :], self.x1_tiles[h, t]).then_inc(self.ring_in[t % 2], 16)

    def first_rows(self, pool, step):
        for w, name in enumerate(("gate", "up")):
            ins = pool.tensor_copy(self.cur_in[:, w, :], self.keep["row_" + name])
        step.mark(ins)

    def gather(self, pool, u):
        slot = SZ_SLOT[u]
        if u in GATES:
            w, quad = GATES[u]
            table, width = self.d[("table_gate", "table_up")[w]], ROW_IN
            rows = [self.cur_in[:, w, k:k + 1] for k in range(QUAD * quad, QUAD * quad + QUAD)]
        else:
            table, width, rows = self.d["table_down"], ROW_DOWN, [self.cur_dn[:, u:u + 1]]
        for i, row in enumerate(rows):
            pool.indirect_dma_start(out=self.sz[slot][:, i * width:(i + 1) * width], out_offset=None, in_=table,
                                    in_offset=bass.IndirectOffsetOnAxis(ap=row, axis=0)).then_inc(self.sz_in[slot], 16)

    def unpack(self, dve, g, u):
        n, slot, s = unit(g, u), u % 2, SZ_SLOT[u]
        step = Steps(dve, self.unit_step, n * 2)
        val, sz = self.wt[:, slot, :], self.sz[s]
        if not (isinstance(n, int) and n < 2):
            dve.wait_ge(self.wlo_done, n - 1)
        if u in GATES:
            w, quad = GATES[u]
            dve.wait_ge(self.qin_in[w], (g + 1) * 16 + 16)
            for i in range(QUAD):
                ins = dve.tensor_scalar(val.bitcast(I32)[:, i * PAIR:(i + 1) * PAIR], self.q_in[:, w, :],
                                        BITS * (QUAD * quad + i), 15, ALU.logical_shift_right, ALU.bitwise_and)
            ints = val.bitcast(I32).rearrange("p (i n) -> p i n", i=QUAD)
            val = val.rearrange("p (i n) -> p i n", i=QUAD)
            scale = sz.rearrange("p (i w) -> p i w", i=QUAD)[:, :, 0:PAIR]
            zero = sz.bitcast(BF16).rearrange("p (i w) -> p i w", i=QUAD)[:, :, 2 * PAIR:3 * PAIR]
        else:
            dve.wait_ge(self.qdn_in[u], g * 16 + 16)
            ins = dve.tensor_scalar(val.bitcast(I32), self.q_dn[:, u, :], self.shift[:, 0:1], 15,
                                    ALU.logical_shift_right, ALU.bitwise_and)
            ints, scale, zero = val.bitcast(I32), sz[:, 0:HID], sz.bitcast(BF16)[:, 2 * HID:3 * HID]
        step.mark(ins)
        step.wait()
        dve.wait_ge(self.sz_in[s], g * SZ_PAIR[s] + (SZ_FIRST[s] + SZ_WITH[u]))
        step.mark(dve.tensor_tensor(val, ints, zero, ALU.subtract))
        step.wait()
        dve.tensor_tensor(val, val, scale, ALU.mult).then_inc(self.w_made, 1)


def phase_mlp(nc, d, ps, keep, sem, feed):
    m = Map(nc, keep["end_const"])
    x_hi, x_lo = m.put("c_x_hi", [P, KT, HALF], F32R), m.put("c_x_lo", [P, KT, HALF], F32R)
    acc = m.put("c_acc", [P, HTT, HID], F32)
    in_hi, in_lo = m.put("c_in_hi", [P, 2, KT, PAIR], F32R), m.put("c_in_lo", [P, 2, KT, PAIR], F32R)
    dn_hi, dn_lo = m.put("c_dn_hi", [P, 2, HID], F32R), m.put("c_dn_lo", [P, 2, HID], F32R)
    h_hi, h_lo = m.put("c_h_hi", [P, 2, HALF], F32R), m.put("c_h_lo", [P, 2, HALF], F32R)
    stats = m.put("c_stats", [P, HTT, NH, 6], F32)
    mv, var_eps, rstd = m.put("c_mv", [P, HTT, 2], F32), m.put("c_var_eps", [P, HTT], F32), m.put("c_rstd", [P, HTT], F32)
    neg_mean = m.put("c_neg_mean", [P, HTT], F32)

    assert m.at <= feed.start
    silu, x_ring, wt = feed.silu, feed.x_ring, feed.wt
    spare = [t.rearrange("p (s k) n -> p s (k n)", s=2).bitcast(F32) for t in (in_hi[:, 1, :, :], in_lo[:, 1, :, :])]
    x0_tiles = [t[:, s, :] for t in (x_ring, *spare, dn_hi[:, :, :].bitcast(F32)) for s in range(2)]
    x0_in = [sem(f"c_x0_in{t}") for t in range(HTT)]
    ring_in, sz_in, row_step, unit_step, w_made, wlo_done = (
        feed.ring_in, feed.sz_in, feed.row_step, feed.unit_step, feed.w_made, feed.wlo_done)
    acc_in = [sem(f"c_acc_in{t}") for t in range(HTT)]
    out_done = [sem(f"c_out_done{t}") for t in range(HTT)]
    ln_step, eps_step, whi_done = sem("c_ln_step"), sem("c_eps_step"), sem("c_whi_done")
    xt_ready, xhi_done, xlo_done = sem("c_xt_ready"), sem("c_xhi_done"), sem("c_xlo_done")
    gate_ready, up_ready = sem("c_gate_ready"), sem("c_up_ready")
    down_ready = sem("c_down_ready")
    silu_done, h_made, hhi_done, hlo_done = sem("c_silu_done"), sem("c_h_made"), sem("c_hhi_done"), sem("c_hlo_done")
    acc_done = sem("c_acc_done")
    var_done, rstd_done, x2_done = sem("c_var_done"), sem("c_rstd_done"), sem("c_x2_done")

    BLK = 2 * HC
    DN = HTT * NH
    XT = HTT * 2
    assert BLK == 4 and DN == 16

    x1_tiles = d["x1_scratch"].rearrange("(h n p) c -> h n p c", h=HALVES, p=P)
    out_tiles = d["out"].rearrange("(h n p) c -> h n p c", h=HALVES, p=P)

    def halves(eng, body):
        for h in range(HALVES):
            with eng.Fori(0, PAIRS - 1) as p:
                body(h, p, p + h * PAIRS, False)
            body(h, PAIRS - 1, h * PAIRS + PAIRS - 1, True)
            yield h

    def more(h, last):
        return not (last and h == HALVES - 1)

    with nc.Block() as block:
        @block.sync
        def _(sp):
            def body(h, p, g, last):
                if more(h, last):
                    for t in range(2):
                        sp.wait_ge(unit_step, unit(g, DN0 + t) * 2 + 1)
                        feed.load_dn(sp, t, p + 1)
                    sp.wait_ge(unit_step, unit(g, GB) * 2 + 1)
                    feed.load_in(sp, 0, p + 2)
                    if last:
                        sp.wait_ge(hlo_done, g * BLK + 2 * BLK)
                        for t in range(HTT):
                            if t >= 2:
                                sp.wait_ge(xt_ready, XT * (h + 1) + 2 * (t - 2) + 2)
                            feed.load_ring(sp, h + 1, t)
                    sp.wait_ge(unit_step, unit(g, UB) * 2 + 1)
                    feed.load_in(sp, 1, p + 2)

            for t in range(2, HTT):
                sp.dma_start(x0_tiles[t], x1_tiles[0, t]).then_inc(x0_in[t], 16)
            sp.wait_ge(unit_step, 2 * 1 + 1)
            feed.load_in(sp, 0, 1)
            sp.wait_ge(unit_step, 2 * 3 + 1)
            feed.load_in(sp, 1, 1)
            for t in range(HTT):
                sp.dma_start(acc[:, t, :], x1_tiles[0, t]).then_inc(acc_in[t], 16)
            for t in range(TT):
                sp.wait_ge(feed.x1_out[t], 16 * (CHUNKS + 1))
            for h in halves(sp, body):
                for t in range(HTT):
                    sp.wait_ge(x2_done, HTT * h + t + 1)
                    sp.dma_start(out_tiles[h, t], acc[:, t, :]).then_inc(out_done[t], 16)
                for t in range(HTT):
                    sp.wait_ge(out_done[t], 16 * (h + 1))
                    if h < HALVES - 1:
                        sp.dma_start(acc[:, t, :], x1_tiles[h + 1, t]).then_inc(acc_in[t], 16)

        @block.gpsimd
        def _(pool):
            def body(h, p, g, last):
                def fetch(u):
                    wait_apart(pool, keep, w_made, unit(g, u) - 2)
                    feed.gather(pool, u)

                step = Steps(pool, row_step, g * 2 + (h + 1))
                for s in (1, 2):
                    pool.wait_ge(sz_in[s], g * SZ_PAIR[s] + SZ_FIRST[s])
                step.mark(pool.tensor_copy(feed.cur_dn[:, :], keep["row_down"][:, bass.ts(p, 2)]))
                step.wait()
                fetch(DN0)
                fetch(DN1)
                wait_apart(pool, keep, sz_in[0], g * SZ_PAIR[0] + SZ_FIRST[0])
                step.mark(pool.tensor_scalar(feed.cur_in[:, :, :], feed.cur_in[:, :, :], 1.0, None, ALU.add))
                step.wait()
                if more(h, last):
                    for u in (GA, GB, UA, UB):
                        fetch(u)

            feed.gather(pool, UA)
            pool.wait_ge(w_made, 1)
            feed.gather(pool, UB)
            for h in halves(pool, body):
                if h < HALVES - 1:
                    for s in range(3):
                        pool.wait_ge(sz_in[s], (h + 1) * PAIRS * SZ_PAIR[s] + SZ_FIRST[s])
                    feed.first_rows(pool, Steps(pool, row_step, 2 * PAIRS * (h + 1) + h + 1))
                step = Steps(pool, eps_step, 3 * HTT * h)
                for t in range(HTT):
                    pool.wait_ge(var_done, HTT * h + t + 1)
                    step.mark(pool.tensor_scalar(var_eps[:, t:t + 1], mv[:, t, 1:2], EPS, None, ALU.add))
                    step.mark(pool.tensor_scalar(neg_mean[:, t:t + 1], mv[:, t, 0:1], -1.0, None, ALU.mult))
                    step.wait()
                    step.mark(pool.tensor_tensor(out=rstd[:, t:t + 1], in0=var_eps[:, t:t + 1],
                                                 in1=keep["minus_half"][:, 0:1], op=ALU.pow))
                    step.wait()
                    pool.tensor_tensor(out=neg_mean[:, t:t + 1], in0=neg_mean[:, t:t + 1], in1=rstd[:, t:t + 1],
                                       op=ALU.mult).then_inc(rstd_done, 1)

        @block.scalar
        def _(act):
            def in_hi_unit(n, w, half):
                out = in_hi[:, w, QUAD * half:QUAD * (half + 1), :].rearrange("p i n -> p (i n)")
                act.wait_ge(w_made, n + 1)
                act.activation(out, wt[:, half, :], ACT.Copy).then_inc(whi_done, 1)

            def x_hi_quad(h, k, bank):
                act.wait_ge(xt_ready, XT * h + k + 1)
                t, quad = k // 2, k % 2
                act.activation(x_hi[:, QUAD * quad:QUAD * (quad + 1), t * P:(t + 1) * P],
                               ps[:, bank, :].rearrange("p (i t) -> p i t", t=P), ACT.Copy).then_inc(xhi_done, 1)

            def body(h, p, g, last):
                for b in range(BLK):
                    act.wait_ge(gate_ready, g * BLK + b + 1)
                    act.wait_ge(hlo_done, g * BLK + b + 1)
                    act.activation(silu[:, b, :], ps[:, b, :], ACT.Silu).then_inc(silu_done, 1)
                    if b < 2:
                        act.wait_ge(w_made, unit(g, DN0 + b) + 1)
                        act.wait_ge(down_ready, g * DN + DN)
                        act.activation(dn_hi[:, b, :], wt[:, b, :], ACT.Copy).then_inc(whi_done, 1)

                def h_high(b):
                    act.wait_ge(h_made, g * BLK + BLK + b + 1)
                    act.activation(h_hi[:, b // HC, (b % HC) * BANK:(b % HC + 1) * BANK], silu[:, b, :], ACT.Copy
                                   ).then_inc(hhi_done, 1)

                if more(h, last):
                    act.wait_ge(gate_ready, g * BLK + BLK)
                    in_hi_unit(unit(g, GA), 0, 0)
                h_high(0)
                if more(h, last):
                    in_hi_unit(unit(g, GB), 0, 1)
                for b in range(1, BLK):
                    h_high(b)
                turned = last and h < HALVES - 1
                if last:
                    for t in range(HTT + 1):
                        if turned and t < HTT:
                            for k in (2 * t, 2 * t + 1):
                                x_hi_quad(h + 1, k, x_bank(k))
                        if t:
                            act.wait_ge(rstd_done, HTT * h + t)
                            act.activation(acc[:, t - 1, :], acc[:, t - 1, :], ACT.Identity, scale=rstd[:, t - 1:t],
                                           bias=neg_mean[:, t - 1:t]).then_inc(x2_done, 1)
                if more(h, last):
                    act.wait_ge(up_ready, g * BLK + BLK)
                    in_hi_unit(unit(g, UA), 1, 0)
                    in_hi_unit(unit(g, UB), 1, 1)

            act.sem_inc(h_made, BLK)
            act.sem_inc(hlo_done, BLK)
            in_hi_unit(0, 0, 0)
            in_hi_unit(1, 0, 1)
            for k in range(XT):
                x_hi_quad(0, k, x0_bank(k))
            in_hi_unit(2, 1, 0)
            in_hi_unit(3, 1, 1)
            for t in range(TT):
                act.wait_ge(feed.x1_out[t], 16 * (CHUNKS + 1))
            for h in halves(act, body):
                pass

        @block.vector
        def _(dve):
            def w_low(n, slot, hi, lo):
                dve.wait_ge(whi_done, n + 1)
                dve.tensor_tensor(lo, wt[:, slot, :], hi.bitcast(F32), ALU.subtract).then_inc(wlo_done, 1)

            def in_low(n, w, half):
                hi, lo = (t[:, w, QUAD * half:QUAD * (half + 1), :].rearrange("p i n -> p (i n)") for t in (in_hi, in_lo))
                w_low(n, half, hi, lo)

            def x_low_quad(h, k, bank):
                dve.wait_ge(xhi_done, XT * h + k + 1)
                t, quad = k // 2, k % 2
                hi, lo = (x[:, QUAD * quad:QUAD * (quad + 1), t * P:(t + 1) * P] for x in (x_hi, x_lo))
                dve.tensor_tensor(lo, ps[:, bank, :].rearrange("p (i t) -> p i t", t=P), hi.bitcast(F32), ALU.subtract
                                  ).then_inc(xlo_done, 1)

            def body(h, p, g, last):
                turned = last and h < HALVES - 1
                step = Steps(dve, ln_step, HTT * h)

                def h_make(b):
                    dve.wait_ge(up_ready, g * BLK + b + 1)
                    dve.wait_ge(silu_done, g * BLK + b + 1)
                    dve.tensor_tensor(silu[:, b, :], silu[:, b, :], ps[:, 4 + b, :], ALU.mult).then_inc(h_made, 1)

                def h_low(b):
                    dve.wait_ge(hhi_done, g * BLK + b + 1)
                    hi, lo = (t[:, b // HC, (b % HC) * BANK:(b % HC + 1) * BANK] for t in (h_hi, h_lo))
                    dve.tensor_tensor(lo, silu[:, b, :], hi.bitcast(F32), ALU.subtract).then_inc(hlo_done, 1)

                def add(n):
                    t, b = n // NH, n % NH
                    part = acc[:, t, b * BANK:(b + 1) * BANK]
                    dve.wait_ge(down_ready, g * DN + DN + n + 1)
                    if b == 0:
                        dve.wait_ge(acc_in[t], 16 * (h + 1))
                    bank = (4 * t + b) % 8 if turned else n % 8
                    dve.tensor_tensor(part, ps[:, bank, :], part, ALU.add).then_inc(acc_done, 1)

                def add_tile(t):
                    for n in range(NH * t, NH * t + NH):
                        add(n)
                    if turned:
                        for k in (2 * t, 2 * t + 1):
                            x_low_quad(h + 1, k, x_bank(k))
                    if last:
                        dve.wait_ge(acc_done, g * DN + DN + NH * (t + 1))
                        layer_norm_steps(dve, keep, acc[:, t, :], stats[:, t, :, :], mv[:, t, :], step, var_done)

                feed.unpack(dve, g, DN0)
                feed.unpack(dve, g, DN1)
                w_low(unit(g, DN0), 0, dn_hi[:, 0, :], dn_lo[:, 0, :])
                w_low(unit(g, DN1), 1, dn_hi[:, 1, :], dn_lo[:, 1, :])
                if more(h, last):
                    feed.unpack(dve, g, GA)
                h_make(0)
                if more(h, last):
                    in_low(unit(g, GA), 0, 0)
                    feed.unpack(dve, g, GB)
                h_make(1)
                h_low(0)
                if more(h, last):
                    in_low(unit(g, GB), 0, 1)
                h_low(1)
                h_make(2)
                h_low(2)
                h_make(3)
                h_low(3)
                if more(h, last):
                    if turned:
                        for t in range(HTT):
                            add_tile(t)
                    feed.unpack(dve, g, UA)
                    if not turned:
                        add_tile(0)
                        add_tile(1)
                    in_low(unit(g, UA), 1, 0)
                    feed.unpack(dve, g, UB)
                    if not turned:
                        add_tile(2)
                        add_tile(3)
                    in_low(unit(g, UB), 1, 1)
                    for t in range(4, 0 if turned else HTT):
                        add_tile(t)
                else:
                    for t in range(HTT):
                        add_tile(t)

            dve.sem_inc(acc_done, DN)
            in_low(0, 0, 0)
            in_low(1, 0, 1)
            for k in range(XT):
                x_low_quad(0, k, x0_bank(k))
            feed.unpack(dve, -1, UA)
            in_low(2, 1, 0)
            feed.unpack(dve, -1, UB)
            in_low(3, 1, 1)
            for h in halves(dve, body):
                pass

        @block.tensor
        def _(pe):
            def turn(h, k, bank):
                t, quad = k // 2, k % 2
                src = x0_tiles[t] if h == 0 else x_ring[:, t % 2, :]
                if quad == 0:
                    if h == 0 and t >= 2:
                        pe.wait_ge(x0_in[t], 16)
                    else:
                        pe.wait_ge(ring_in[t % 2], 16 * (1 if h == 0 else HTT // 2 * (h - 1) + t // 2 + 2))
                cols = src.rearrange("p (r i) -> p i r", i=PACK)
                for i in range(QUAD):
                    tr = pe.transpose(ps[:, bank, i * P:(i + 1) * P], cols[:, QUAD * quad + i, :], keep["ident"][:, :])
                tr.then_inc(xt_ready, 1)

            def body(h, p, g, last):
                turned = last and h < HALVES - 1
                for w, ready in ((0, gate_ready), (1, up_ready)):
                    for j in range(2):
                        for c in range(HC):
                            b = HC * j + c
                            pe.wait_ge(acc_done, g * DN + 8 + 4 * w + b + 1)
                            for i in range(KT):
                                if i == 0 and b < HC and w == 0:
                                    pe.wait_ge(xlo_done, XT * h + 2 * TT * (c + 1))
                                if b == 0 and i % QUAD == 0:
                                    pe.wait_ge(wlo_done, g * UNITS + 2 * w + i // QUAD + 1)
                                cols, toks = slice(j * P, (j + 1) * P), slice(c * BANK, (c + 1) * BANK)
                                mm = three_pass(pe, ps[:, 4 * w + b, :], (in_hi[:, w, i, cols], in_lo[:, w, i, cols]),
                                                (x_hi[:, i, toks], x_lo[:, i, toks]), i == 0, i == KT - 1)
                            mm.then_inc(ready, 1)
                pe.wait_ge(wlo_done, unit(g, DN1) + 1)
                for t in range(HTT):
                    if t % TT == 0:
                        pe.wait_ge(hlo_done, g * BLK + BLK + HC + t // TT + 1)
                    for b in range(NH):
                        n, e = NH * t + b, 4 * t + b if turned else NH * t + b
                        bank = e % 8
                        if e < 4:
                            pe.wait_ge(silu_done, g * BLK + bank + 1)
                        elif e < 8:
                            pe.wait_ge(h_made, g * BLK + BLK + bank - 4 + 1)
                        else:
                            pe.wait_ge(acc_done, g * DN + DN + (n - 4 if turned else n - 8) + 1)
                        for j in range(2):
                            toks, cols = slice(t * P, (t + 1) * P), slice(b * BANK, (b + 1) * BANK)
                            mm = three_pass(pe, ps[:, bank, :], (h_hi[:, j, toks], h_lo[:, j, toks]),
                                            (dn_hi[:, j, cols], dn_lo[:, j, cols]), j == 0, j == 1)
                        mm.then_inc(down_ready, 1)
                    if turned:
                        for k in (2 * t, 2 * t + 1):
                            if t == 0:
                                pe.wait_ge(silu_done, g * BLK + x_bank(k) + 1)
                            elif t == 1:
                                pe.wait_ge(h_made, g * BLK + BLK + x_bank(k) - 4 + 1)
                            else:
                                pe.wait_ge(xlo_done, XT * (h + 1) + k - 4 + 1)
                            turn(h + 1, k, x_bank(k))

            pe.sem_inc(down_ready, DN)
            for k in range(XT):
                if k >= 8:
                    pe.wait_ge(xlo_done, k - 4 + 1)
                turn(0, k, x0_bank(k))
            for h in halves(pe, body):
                if h < HALVES - 1:
                    pe.wait_ge(acc_done, DN * PAIRS * (h + 1) + 14)
                    pe.wait_ge(xlo_done, XT * (h + 1) + 14)


def x0_bank(k):
    return k if k < 8 else 4 + k % 4


def x_bank(k):
    return (4 * (k // 2) + 2 + k % 2) % 8


def build(nc, d, out):
    d["out"] = out
    sems = {}

    def sem(name):
        sems[name] = nc.alloc_semaphore(name)
        return sems[name]

    d["q_scratch"] = nc.dram_tensor("q_scratch", (CHUNKS, P, 2 * HT * CHUNK), F32).ap()
    d["x1_scratch"] = nc.dram_tensor("x1_scratch", (TOKENS, HID), F32).ap()
    d["table_gate"] = nc.dram_tensor("table_gate", (GROUPS_IN * BLOCKS, ROW_IN), F32).ap()
    d["table_up"] = nc.dram_tensor("table_up", (GROUPS_IN * BLOCKS, ROW_IN), F32).ap()
    d["table_down"] = nc.dram_tensor("table_down", (GROUPS_DOWN, ROW_DOWN), F32).ap()

    m = Map(nc, SBUF_FIRST)
    ident, minus_half = m.put("ident", [P, P], F32), m.put("minus_half", [P, 1], F32)
    keep = {"ident": ident, "minus_half": minus_half, "const": sem("const")}
    for name, n in (("gate", KT), ("up", KT), ("down", 2 * PAIRS)):
        keep["row_" + name] = m.put("row_" + name, [P, n], I32)[:, :]
    keep["end_const"] = m.at
    for name in ("k_hi", "k_lo"):
        keep[name] = m.put(name, [P, HT, TOKENS], F32R)
    for name in ("v_hi", "v_lo"):
        keep[name] = m.put(name, [P, NKEY, HEAD], F32R)
    keep["end"] = m.at
    keep["q_hl"] = m.put("b_q_hl", [P, 2, HT, CHUNK], F32R)
    keep["q_in"], keep["end_q"] = sem("b_q_in"), m.at
    with nc.psum_tensor("ps", [P, 8, BANK], F32) as ps:
        phase_qkv(nc, d, ps, keep, sem)
        feed = Feed(nc, d, keep, sem)
        phase_attention(nc, d, ps, keep, sem, feed)
        phase_mlp(nc, d, ps, keep, sem, feed)


def _blocks(a, wrap):
    out = np.zeros((P, PAIRS, PAIR), a.dtype)
    out.reshape(P, INTER_PAD)[:, :INTER] = a
    out = out.transpose(1, 0, 2)
    return np.ascontiguousarray(np.concatenate([out, out[:wrap]]))


def _wide(a, n, axis):
    shape = list(a.shape)
    shape[axis] = n
    out = np.zeros(shape, a.dtype)
    out[tuple(slice(0, s) for s in a.shape)] = a
    return out


def kernel(**inputs):
    import concourse.bacc as bacc
    from concourse.bass_utils import run_bass_kernel_spmd

    a = {k.removeprefix("L0_"): np.asarray(v) for k, v in inputs.items()}
    x = a["attn_x"].reshape(TOKENS, HID)
    q_down = _wide(a["ffn_down_qweight"], (PAIRS + 1) * PAIR // PACK, 0)
    q_down[PAIRS * PAIR // PACK:] = q_down[:PAIR // PACK]
    arrays = {
        "x": x,
        "xT": np.ascontiguousarray(x.T),
        "Wqkv": a["attn_Wqkv"],
        "bias_qk": np.ascontiguousarray(a["attn_bqkv"][:2 * HEAD].reshape(2 * HT, P).T),
        "bias_v": a["attn_bqkv"][2 * HEAD:].reshape(1, HEAD),
        "Wo": a["attn_Wo"],
        "bo": a["attn_bo"].reshape(1, HID),
        "q_gate": _blocks(a["ffn_gate_qweight"], 2),
        "q_up": _blocks(a["ffn_up_qweight"], 2),
        "q_down": q_down,
        "scales_gate": _wide(a["ffn_gate_scales"], INTER_PAD, 1),
        "scales_up": _wide(a["ffn_up_scales"], INTER_PAD, 1),
        "scales_down": a["ffn_down_scales"],
        "zeros_gate": _wide(a["ffn_gate_qzeros"], INTER_PAD // PACK, 1),
        "zeros_up": _wide(a["ffn_up_qzeros"], INTER_PAD // PACK, 1),
        "zeros_down": a["ffn_down_qzeros"],
        "g_idx_gate": a["ffn_gate_g_idx"].reshape(P, KT),
        "g_idx_up": a["ffn_up_g_idx"].reshape(P, KT),
        "g_idx_down": np.ascontiguousarray(_wide(a["ffn_down_g_idx"], INTER_PAD, 0).reshape(2 * PAIRS, P).T),
        "shift": np.tile(np.arange(0, 32, BITS, dtype=np.int32), P // PACK).reshape(P, 1),
    }
    arrays = {k: np.ascontiguousarray(v) for k, v in arrays.items()}

    nc = bacc.Bacc("TRN2", target_bir_lowering=False, num_devices=1)
    d = {k: nc.dram_tensor(k, v.shape, mybir.dt.from_np(v.dtype), kind="ExternalInput").ap() for k, v in arrays.items()}
    out = nc.dram_tensor("out", (TOKENS, HID), F32, kind="ExternalOutput").ap()
    build(nc, d, out)
    r = run_bass_kernel_spmd(nc, [arrays], core_ids=[0])
    return r.results[0]["out"].reshape(1, TOKENS, HID)
```

```python
import numpy as np

import concourse.bass as bass
from concourse import mybir
from concourse.alu_op_type import AluOpType as ALU

ACT = mybir.ActivationFunctionType
F32 = mybir.dt.float32
F32R = mybir.dt.float32r
BF16 = mybir.dt.bfloat16
I32 = mybir.dt.int32
AX_X = mybir.AxisListType.X

P = 128
BANK = 512
TOKENS, HID, HEAD, INTER = 2048, 1024, 256, 2752
PACK, BITS = 8, 4
EPS = 1e-5

CHUNK = 512
CHUNKS = TOKENS // CHUNK
TT = CHUNK // P
KT = HID // P
HT = HEAD // P
NKEY = TOKENS // P
KB = TOKENS // BANK
NH = HID // BANK

HALF = TOKENS // 2
HALVES = TOKENS // HALF
HC = HALF // BANK
HTT = HALF // P
PAIR = 2 * P
PAIRS = -(-INTER // PAIR)
REST = INTER % P
assert 0 < REST <= P // 2 and (INTER - REST) // P % 2
INTER_PAD = PAIRS * PAIR
GROUPS_IN = HID // 128
GROUPS_DOWN = INTER // 128
BLOCKS = PAIRS + 1
ROW_IN = PAIR + PAIR // 2
ROW_DOWN = HID + HID // 2
QUAD = 4
UNIT = QUAD * PAIR
assert UNIT == HID and QUAD * ROW_IN == ROW_DOWN

SBUF_FIRST = 16512


class Map:

    def __init__(self, nc, at):
        self.nc, self.at = nc, at

    def put(self, name, shape, dtype):
        t = self.nc.alloc_sbuf_tensor_at(name, shape, dtype, offset=self.at)
        self.at += -(-int(np.prod(shape[1:])) * (2 if dtype == BF16 else 4) // 32) * 32
        assert self.at <= self.nc.sbuf_usable_end, (name, self.at)
        return t


class Steps:

    def __init__(self, eng, sem, value):
        self.eng, self.sem, self.value = eng, sem, value

    def mark(self, ins):
        ins.then_inc(self.sem, 1)
        self.value = self.value + 1

    def wait(self):
        self.eng.wait_ge(self.sem, self.value)


def wait_apart(eng, keep, sem, value):
    value = value if isinstance(value, int) else eng.to_reg(value)
    eng.wait_ge(keep["const"], 3)
    eng.wait_ge(sem, value)


def three_pass(pe, out, lhs, rhs, first, last):
    pe.matmul(out, lhs[0], rhs[0], start=first, stop=False)
    pe.matmul(out, lhs[0], rhs[1], start=False, stop=False)
    return pe.matmul(out, lhs[1], rhs[0], start=False, stop=last)


def transpose_quad(pe, keep, out, tile, quad):
    cols = tile.rearrange("p (r i) -> p i r", i=PACK)
    for i in range(QUAD):
        tr = pe.transpose(out[:, i * P:(i + 1) * P], cols[:, QUAD * quad + i, :], keep["ident"][:, :])
    return tr


def phase_qkv(nc, d, ps, keep, sem):
    m = Map(nc, keep["end"])
    w_f32 = m.put("a_w_f32", [P, KT, 3 * HEAD], F32)
    w_hi = m.put("a_w_hi", [P, KT, 3 * HEAD], F32R)
    w_lo = m.put("a_w_lo", [P, KT, 3 * HEAD], F32R)
    x_f32 = m.put("a_x_f32", [P, KT, CHUNK], F32)
    x_hi = m.put("a_x_hi", [P, KT, CHUNK], F32R)
    x_lo = m.put("a_x_lo", [P, KT, CHUNK], F32R)
    q_hl = m.put("a_q_hl", [P, 2, HT, CHUNK], F32R)
    v_f32 = m.put("a_v_f32", [P, TT, HEAD], F32)
    bias_col = m.put("a_bias_col", [P, 2 * HT], F32)
    bias_v = m.put("a_bias_v", [P, HEAD], F32)
    zp = {"gate": m.put("a_zp_gate", [P, INTER_PAD // PACK], I32), "up": m.put("a_zp_up", [P, INTER_PAD // PACK], I32),
          "down": m.put("a_zp_down", [P, HID // PACK], I32)}
    g_idx = {"gate": m.put("a_g_gate", [P, KT], I32), "up": m.put("a_g_up", [P, KT], I32),
             "down": m.put("a_g_down", [P, 2 * PAIRS], I32)}
    gi_a, gi_b = m.put("a_gi_a", [P, 2 * PAIRS], F32), m.put("a_gi_b", [P, 2 * PAIRS], F32)
    zbf = {"down": m.put("a_zbf_down", [P, HID], BF16)}
    m = Map(nc, keep["end"])
    znib = m.put("a_znib", [P, INTER_PAD // PACK, PACK], I32)
    zbf["gate"] = m.put("a_zbf_gate", [P, INTER_PAD], BF16)
    zbf["up"] = m.put("a_zbf_up", [P, INTER_PAD], BF16)
    assert m.at <= keep["end"] + 4 * KT * 3 * HEAD
    tab_in, tab_out, z_done = sem("a_tab_in"), sem("a_tab_out"), sem("a_z_done")
    k_hi, k_lo, v_hi, v_lo = keep["k_hi"], keep["k_lo"], keep["v_hi"], keep["v_lo"]

    bias_in = sem("a_bias_in")
    w_in = [sem(f"a_w_in{k}") for k in range(KT)]
    x_in = [sem(f"a_x_in{k}") for k in range(KT)]
    q_out = sem("a_q_out")
    whi_done, wlo_done = sem("a_whi_done"), sem("a_wlo_done")
    xhi_done, xlo_done = sem("a_xhi_done"), sem("a_xlo_done")
    x_used = sem("a_x_used")
    qk_ready, v_ready = sem("a_qk_ready"), sem("a_v_ready")
    qkhi_done = sem("a_qkhi_done")
    qklo_done = sem("a_qklo_done")
    v_done = sem("a_v_done")
    vhi_done = sem("a_vhi_done")
    vlo_done = sem("a_vlo_done")

    x_src = d["xT"].rearrange("(k p) t -> k p t", p=P)
    w_src = d["Wqkv"].rearrange("(k p) f -> k p f", p=P)
    q_dst = d["q_scratch"]

    def unpack_zeros(dve, step):
        for n, (name, groups) in enumerate((("gate", GROUPS_IN), ("up", GROUPS_IN), ("down", GROUPS_DOWN))):
            words = zp[name].shape[1]
            if n:
                dve.wait_ge(z_done, n)
            for j in range(PACK):
                ins = dve.tensor_scalar(znib[0:groups, 0:words, j], zp[name][0:groups, :], BITS * j, 15,
                                        ALU.logical_shift_right, ALU.bitwise_and)
            step.mark(ins)
            step.wait()
            dve.tensor_scalar(zbf[name][0:groups, :], znib[0:groups, 0:words, :].rearrange("g w j -> g (w j)"),
                              1.0, None, ALU.add).then_inc(z_done, 1)

    def form_rows(dve, step):
        for name, groups, stride in (("gate", GROUPS_IN, BLOCKS), ("up", GROUPS_IN, BLOCKS), ("down", GROUPS_DOWN, 1)):
            g, out = g_idx[name], keep["row_" + name]
            a, b = gi_a[:, 0:g.shape[1]], gi_b[:, 0:g.shape[1]]
            for make in (lambda: dve.tensor_copy(a, g[:, :]),
                         lambda: dve.tensor_scalar(b, a, 0.0, float(groups), ALU.is_lt, ALU.mult),
                         lambda: dve.tensor_tensor(b, a, b, ALU.add),
                         lambda: dve.tensor_scalar(a, b, 0.0, float(groups - 1), ALU.max, ALU.min),
                         lambda: dve.tensor_scalar(out, a, float(stride), None, ALU.mult)):
                step.mark(make())
                step.wait()

    with nc.Block() as block:
        @block.sync
        def _(sp):
            for k in range(KT):
                sp.dma_start(x_f32[:, k, :], x_src[k][:, 0:CHUNK]).then_inc(x_in[k], 16)
                sp.dma_start(w_f32[:, k, :], w_src[k]).then_inc(w_in[k], 16)
            sp.dma_start(bias_col[:, :], d["bias_qk"]).then_inc(bias_in, 16)
            sp.dma_start(bias_v[:, :], d["bias_v"].to_broadcast([P, HEAD])).then_inc(bias_in, 16)

            def chunk(c, fetch):
                if fetch:
                    for k in range(KT):
                        sp.wait_ge(xlo_done, KT * c + k + 1)
                        sp.dma_start(x_f32[:, k, :], x_src[k][:, bass.ts(c + 1, CHUNK)]).then_inc(x_in[k], 16)
                sp.wait_ge(qklo_done, 4 * c + 4 + 2)
                sp.dma_start(q_dst[c], q_hl[:, :, :, :].rearrange("p s h t -> p (s h t)").bitcast(F32)
                             ).then_inc(q_out, 16)

            with sp.Fori(0, CHUNKS - 1) as c:
                chunk(c, True)
            sp.wait_ge(z_done, 3)
            sp.wait_ge(q_out, 16 * CHUNKS)
            sp.dma_start(keep["q_hl"][:, :, :, :].rearrange("p s h t -> p (s h t)").bitcast(F32), q_dst[0]
                         ).then_inc(keep["q_in"], 16)
            chunk(CHUNKS - 1, False)
            sp.wait_ge(q_out, 16 * (CHUNKS + 1))

        @block.gpsimd
        def _(pool):
            for name, groups in (("gate", GROUPS_IN), ("up", GROUPS_IN), ("down", GROUPS_DOWN)):
                pool.dma_start(zp[name][0:groups, :], d["zeros_" + name]).then_inc(tab_in, 16)
                pool.dma_start(g_idx[name][:, :], d["g_idx_" + name]).then_inc(tab_in, 16)
            for name in ("gate", "up"):
                tab = d["table_" + name].rearrange("(g b) w -> g b w", b=BLOCKS)
                src = d["scales_" + name].rearrange("g (b n) -> g b n", n=PAIR)
                pool.dma_start(tab[:, 0:PAIRS, 0:PAIR], src).then_inc(tab_out, 16)
                pool.dma_start(tab[:, PAIRS:BLOCKS, 0:PAIR], src[:, 0:1, :]).then_inc(tab_out, 16)
            pool.dma_start(d["table_down"][:, 0:HID], d["scales_down"]).then_inc(tab_out, 16)
            pool.memset(keep["ident"][:, :], 0.0).then_inc(keep["const"], 1)
            pool.memset(keep["minus_half"][:, :], -0.5).then_inc(keep["const"], 1)
            pool.wait_ge(keep["const"], 2)
            pool.affine_select(out=keep["ident"][:, :], in_=keep["ident"][:, :], compare_op=ALU.not_equal, fill=1.0,
                               base=0, pattern=[[-1, P]], channel_multiplier=1).then_inc(keep["const"], 1)
            for n, name in enumerate(("gate", "up")):
                pool.wait_ge(z_done, n + 1)
                tab = d["table_" + name].rearrange("(g b) w -> g b w", b=BLOCKS)
                src = zbf[name][0:GROUPS_IN, :].bitcast(F32).rearrange("g (b n) -> g b n", n=PAIR // 2)
                pool.dma_start(tab[:, 0:PAIRS, PAIR:ROW_IN], src).then_inc(tab_out, 16)
                pool.dma_start(tab[:, PAIRS:BLOCKS, PAIR:ROW_IN], src[:, 0:1, :]).then_inc(tab_out, 16)
            pool.wait_ge(z_done, 3)
            pool.dma_start(d["table_down"][:, HID:ROW_DOWN], zbf["down"][0:GROUPS_DOWN, 0:HID].bitcast(F32)
                           ).then_inc(tab_out, 16)
            pool.wait_ge(tab_out, 16 * 10)

        @block.scalar
        def _(act):
            for k in range(KT):
                act.wait_ge(x_in[k], 16)
                act.activation(x_hi[:, k, :], x_f32[:, k, :], ACT.Copy).then_inc(xhi_done, 1)
                act.wait_ge(w_in[k], 16)
                act.activation(w_hi[:, k, :], w_f32[:, k, :], ACT.Copy).then_inc(whi_done, 1)
            act.wait_ge(bias_in, 32)

            def chunk(c, fetch):
                for f in range(4):
                    act.wait_ge(qk_ready, 4 * c + f + 1)
                    if f < HT:
                        act.wait_ge(q_out, 16 * c + 16)
                        out = q_hl[:, 0, f, :]
                    else:
                        out = k_hi[:, f - HT, bass.ts(c, CHUNK)]
                    act.activation(out, ps[:, f, :], ACT.Identity, bias=bias_col[:, f:f + 1]).then_inc(qkhi_done, 1)
                if fetch:
                    for k in range(KT):
                        act.wait_ge(x_in[k], 16 * c + 32)
                        if k < KT - 1:
                            act.wait_ge(x_used, (KT - 1) * c + k + 1)
                        else:
                            act.wait_ge(v_ready, TT * c + TT)
                        act.activation(x_hi[:, k, :], x_f32[:, k, :], ACT.Copy).then_inc(xhi_done, 1)
                for t in range(TT):
                    act.wait_ge(v_done, TT * c + TT + t + 1)
                    act.activation(v_hi[:, bass.ds(c * TT + t, 1), :].rearrange("p a h -> p (a h)"),
                                   v_f32[:, t, :], ACT.Copy).then_inc(vhi_done, 1)

            act.sem_inc(q_out, 16)
            with act.Fori(0, CHUNKS - 1) as c:
                chunk(c, True)
            chunk(CHUNKS - 1, False)

        @block.vector
        def _(dve):
            dve.sem_inc(qklo_done, 4)
            dve.sem_inc(v_done, TT)
            for k in range(KT):
                dve.wait_ge(xhi_done, k + 1)
                dve.tensor_tensor(x_lo[:, k, :], x_f32[:, k, :], x_hi[:, k, :].bitcast(F32), ALU.subtract
                                  ).then_inc(xlo_done, 1)
                dve.wait_ge(whi_done, k + 1)
                dve.tensor_tensor(w_lo[:, k, :], w_f32[:, k, :], w_hi[:, k, :].bitcast(F32), ALU.subtract
                                  ).then_inc(wlo_done, 1)
            dve.wait_ge(tab_in, 16 * 6)
            dve.wait_ge(wlo_done, KT)
            step = Steps(dve, sem("a_step"), 0)
            unpack_zeros(dve, step)
            form_rows(dve, step)
            dve.wait_ge(bias_in, 32)

            def chunk(c, fetch):
                for f in range(4):
                    dve.wait_ge(qkhi_done, 4 * c + f + 1)
                    if f < HT:
                        hi, lo = q_hl[:, 0, f, :], q_hl[:, 1, f, :]
                    else:
                        hi, lo = (t[:, f - HT, bass.ts(c, CHUNK)] for t in (k_hi, k_lo))
                    dve.scalar_tensor_tensor(out=lo, in0=ps[:, f, :], scalar=bias_col[:, f:f + 1], in1=hi.bitcast(F32),
                                             op0=ALU.add, op1=ALU.subtract).then_inc(qklo_done, 1)
                if fetch:
                    for k in range(KT):
                        dve.wait_ge(xhi_done, KT * (c + 1) + k + 1)
                        dve.tensor_tensor(x_lo[:, k, :], x_f32[:, k, :], x_hi[:, k, :].bitcast(F32), ALU.subtract
                                          ).then_inc(xlo_done, 1)
                for t in range(TT):
                    dve.wait_ge(v_ready, TT * c + t + 1)
                    dve.wait_ge(vlo_done, TT * c + t + 1)
                    dve.tensor_tensor(v_f32[:, t, :], ps[:, 4 + t, 0:HEAD], bias_v[:, :], ALU.add).then_inc(v_done, 1)
                for t in range(TT):
                    dve.wait_ge(vhi_done, TT * c + t + 1)
                    tile = bass.ds(c * TT + t, 1)
                    dve.tensor_tensor(v_lo[:, tile, :].rearrange("p a h -> p (a h)"), v_f32[:, t, :],
                                      v_hi[:, tile, :].rearrange("p a h -> p (a h)").bitcast(F32), ALU.subtract
                                      ).then_inc(vlo_done, 1)

            dve.sem_inc(vlo_done, TT)
            with dve.Fori(0, CHUNKS - 1) as c:
                chunk(c, True)
            chunk(CHUNKS - 1, False)

        @block.tensor
        def _(pe):
            with pe.Fori(0, CHUNKS) as c:
                for k in range(KT):
                    pe.wait_ge(wlo_done, k + 1)
                    pe.wait_ge(xlo_done, KT * c + k + 1)
                    for f in range(4):
                        if k == 0:
                            pe.wait_ge(qklo_done, 4 * c + f + 1)
                        col = slice(f * P, (f + 1) * P)
                        mm = three_pass(pe, ps[:, f, :], (w_hi[:, k, col], w_lo[:, k, col]),
                                        (x_hi[:, k, :], x_lo[:, k, :]), k == 0, k == KT - 1)
                        if k == KT - 1:
                            mm.then_inc(qk_ready, 1)
                for k in range(KT):
                    for t in range(TT):
                        if k == 0:
                            pe.wait_ge(v_done, TT * c + t + 1)
                        tok, col = slice(t * P, (t + 1) * P), slice(2 * HEAD, 3 * HEAD)
                        mm = three_pass(pe, ps[:, 4 + t, 0:HEAD], (x_hi[:, k, tok], x_lo[:, k, tok]),
                                        (w_hi[:, k, col], w_lo[:, k, col]), k == 0, k == KT - 1)
                        if k == KT - 1 and t < TT - 1:
                            mm.then_inc(v_ready, 1)
                    mm.then_inc(x_used if k < KT - 1 else v_ready, 1)


def layer_norm_steps(dve, keep, x, stats, mv, step, var_done):
    for h in range(NH):
        ins = dve.bn_stats(stats[:, h, :], x[:, h * BANK:(h + 1) * BANK])
    step.mark(ins)
    wait_apart(dve, keep, step.sem, step.value)
    dve.bn_aggr(mv, stats[:, :, :].rearrange("p h s -> p (h s)")).then_inc(var_done, 1)


def rstd_steps(pool, mv, var_eps, rstd, neg_mean, minus_half, step, done):
    step.mark(pool.tensor_scalar(var_eps, mv[:, 1:2], EPS, None, ALU.add))
    step.mark(pool.tensor_scalar(neg_mean, mv[:, 0:1], -1.0, None, ALU.mult))
    step.wait()
    step.mark(pool.tensor_tensor(out=rstd, in0=var_eps, in1=minus_half, op=ALU.pow))
    step.wait()
    pool.tensor_tensor(out=neg_mean, in0=neg_mean, in1=rstd, op=ALU.mult).then_inc(done, 1)


def phase_attention(nc, d, ps, keep, sem, feed):
    m = Map(nc, keep["end_q"])
    wo_hi, wo_lo = m.put("b_wo_hi", [P, HT, HID], F32R), m.put("b_wo_lo", [P, HT, HID], F32R)
    bo = m.put("b_bo", [P, HID], F32)
    prob = m.put("b_prob", [P, TT, TOKENS], F32)
    RING = 4
    pt_hi, pt_lo = m.put("b_pt_hi", [P, RING, CHUNK], F32R), m.put("b_pt_lo", [P, RING, CHUNK], F32R)
    x = m.put("b_x", [P, TT, HID], F32)
    wo_f32 = Map(nc, m.at).put("b_wo_f32", [P, HT, HID], F32)
    o_hi, o_lo = m.put("b_o_hi", [P, HT, CHUNK], F32R), m.put("b_o_lo", [P, HT, CHUNK], F32R)
    neg_max, neg_bias = m.put("b_neg_max", [P, TT], F32), m.put("b_neg_bias", [P, TT], F32)
    row_sum, row_inv = m.put("b_row_sum", [P, TT], F32), m.put("b_row_inv", [P, TT], F32)
    stats = m.put("b_stats", [P, TT, NH, 6], F32)
    mv, var_eps, rstd = m.put("b_mv", [P, TT, 2], F32), m.put("b_var_eps", [P, TT], F32), m.put("b_rstd", [P, TT], F32)
    neg_mean = m.put("b_neg_mean", [P, TT], F32)
    assert m.at <= feed.start_b
    k_hi, k_lo, v_hi, v_lo = keep["k_hi"], keep["k_lo"], keep["v_hi"], keep["v_lo"]
    q_hl, q_in = keep["q_hl"], keep["q_in"]
    scale = float(HEAD) ** -0.5

    wo_in = sem("b_wo_in")
    x_in = [sem(f"b_x_in{t}") for t in range(TT)]
    x1_out = feed.x1_out
    wohi_done, wolo_done = sem("b_wohi_done"), sem("b_wolo_done")
    scores_ready = sem("b_scores_ready")
    bias_ready, exp_done = sem("b_bias_ready"), sem("b_exp_done")
    pt_ready, pthi_done, ptlo_done, pv_done = (sem(n) for n in ("b_pt_ready", "b_pthi_done", "b_ptlo_done", "b_pv_done"))
    o_ready, ohi_done, olo_done = sem("b_o_ready"), sem("b_ohi_done"), sem("b_olo_done")
    proj_ready = sem("b_proj_ready")
    proj_added = sem("b_proj_added")
    bo_added, var_done, rstd_done, x1_done = (sem(n) for n in ("b_bo_added", "b_var_done", "b_rstd_done", "b_x1_done"))
    step_sem, eps_sem = sem("b_step"), sem("b_eps_step")

    x_tiles = d["x"].rearrange("(n p) h -> n p h", p=P)
    x1_tiles = d["x1_scratch"].rearrange("(n p) h -> n p h", p=P)

    def pt_bank(k):
        return (4, 5, 0)[k % 3]

    with nc.Block() as block:
        @block.sync
        def _(sp):
            sp.dma_start(wo_f32[:, :, :], d["Wo"].rearrange("(h p) n -> p h n", p=P)).then_inc(wo_in, 16)
            sp.dma_start(bo[:, :], d["bo"].to_broadcast([P, HID])).then_inc(wo_in, 16)
            for t in range(TT):
                sp.sem_inc(x1_out[t], 16)
            sp.dma_start(feed.shift[:, :], d["shift"]).then_inc(feed.shift_in, 16)
            for w in range(2):
                feed.load_in(sp, w, 0)
            for t in range(2):
                feed.load_dn(sp, t, 0)

            def chunk(c, last=False):
                for t in range(TT):
                    sp.wait_ge(x1_out[t], 16 * c + 16)
                    sp.dma_start(x[:, t, :], x_tiles[c * TT + t]).then_inc(x_in[t], 16)
                if last:
                    sp.wait_ge(pt_ready, NKEY * CHUNKS)
                    for t in range(2, HTT):
                        if t == 4:
                            sp.wait_ge(o_ready, CHUNKS)
                        feed.load_x0(sp, t)
                for t in range(TT):
                    sp.wait_ge(x1_done, TT * c + t + 1)
                    sp.dma_start(x1_tiles[c * TT + t], x[:, t, :]).then_inc(x1_out[t], 16)

            with sp.Fori(0, CHUNKS - 1) as c:
                chunk(c)
            for t in range(2):
                feed.load_x0(sp, t)
            chunk(CHUNKS - 1, last=True)

        @block.gpsimd
        def _(pool):
            rows = Steps(pool, feed.row_step, 0)
            feed.first_rows(pool, rows)
            rows.wait()
            for u in (GA, GB):
                feed.gather(pool, u)
            pool.wait_ge(wo_in, 32)
            with pool.Fori(0, CHUNKS) as c:
                for t in range(TT):
                    pool.wait_ge(x_in[t], 16 * c + 16)
                    pool.tensor_tensor(out=x[:, t, :], in0=x[:, t, :], in1=bo[:, :], op=ALU.add).then_inc(bo_added, 1)
                step = Steps(pool, eps_sem, 3 * TT * c)
                for t in range(TT):
                    wait_apart(pool, keep, var_done, TT * c + t + 1)
                    rstd_steps(pool, mv[:, t, :], var_eps[:, t:t + 1], rstd[:, t:t + 1], neg_mean[:, t:t + 1],
                               keep["minus_half"][:, 0:1], step, rstd_done)

        @block.scalar
        def _(act):

            def normalise(j, t):
                act.wait_ge(rstd_done, TT * j + t + 1)
                act.activation(x[:, t, :], x[:, t, :], ACT.Identity, scale=rstd[:, t:t + 1], bias=neg_mean[:, t:t + 1]
                               ).then_inc(x1_done, 1)

            def chunk(c, first=False, fetch=True):
                for t in range(TT):
                    act.wait_ge(bias_ready, TT * c + t + 1)
                    bank = KB * (t % 2)
                    act.activation(prob[:, t, :], ps[:, bank:bank + KB, :].rearrange("p b n -> p (b n)"), ACT.Exp,
                                   bias=neg_bias[:, t:t + 1], scale=scale, accum_out=row_sum[:, t:t + 1]
                                   ).then_inc(exp_done, 1)
                if first:
                    act.wait_ge(wo_in, 32)
                    for h in range(HT):
                        act.activation(wo_hi[:, h, :], wo_f32[:, h, :], ACT.Copy).then_inc(wohi_done, 1)
                if fetch:
                    act.wait_ge(scores_ready, TT * c + TT)
                    act.dma_start(q_hl[:, :, :, :].rearrange("p s h t -> p (s h t)").bitcast(F32),
                                  d["q_scratch"][c + 1]).then_inc(q_in, 16)
                for k in range(NKEY):
                    act.wait_ge(pt_ready, NKEY * c + k + 1)
                    if k >= RING:
                        act.wait_ge(pv_done, (NKEY - 1) * c + k - RING + 1)
                    act.activation(pt_hi[:, k % RING, :], ps[:, pt_bank(k), :], ACT.Copy).then_inc(pthi_done, 1)
                    if not first and 4 <= k < 4 + TT:
                        normalise(c - 1, k - 4)
                for h in range(HT):
                    act.wait_ge(o_ready, c + 1)
                    act.activation(o_hi[:, h, :], ps[:, 6 + h, :], ACT.Copy).then_inc(ohi_done, 1)

            chunk(0, first=True)
            with act.Fori(0, CHUNKS - 2) as i:
                chunk(i + 1)
            chunk(CHUNKS - 1, fetch=False)
            for t in range(TT):
                normalise(CHUNKS - 1, t)

        @block.vector
        def _(dve):
            dve.sem_inc(proj_added, TT)

            def low(c, k):
                dve.wait_ge(pthi_done, NKEY * c + k + 1)
                dve.tensor_tensor(pt_lo[:, k % RING, :], ps[:, pt_bank(k), :], pt_hi[:, k % RING, :].bitcast(F32),
                                  ALU.subtract).then_inc(ptlo_done, 1)

            def add(j, t):
                dve.wait_ge(proj_ready, TT * j + t + 1)
                dve.wait_ge(bo_added, TT * j + t + 1)
                bank = NH * (t % 2)
                dve.scalar_tensor_tensor(out=x[:, t, :], in0=ps[:, bank:bank + NH, :].rearrange("p b n -> p (b n)"),
                                         scalar=row_inv[:, t:t + 1], in1=x[:, t, :], op0=ALU.mult, op1=ALU.add
                                         ).then_inc(proj_added, 1)

            def statistics(j, t, step):
                dve.wait_ge(proj_added, TT * j + TT + t + 1)
                layer_norm_steps(dve, keep, x[:, t, :], stats[:, t, :, :], mv[:, t, :], step, var_done)

            def chunk(c, step):
                first = isinstance(c, int)
                for t in range(TT):
                    dve.wait_ge(scores_ready, TT * c + t + 1)
                    bank = KB * (t % 2)
                    step.mark(dve.tensor_reduce(neg_max[:, t:t + 1], ps[:, bank:bank + KB, :].rearrange("p b n -> p (b n)"),
                                                AX_X, ALU.max, negate=True))
                    step.wait()
                    dve.tensor_scalar(neg_bias[:, t:t + 1], neg_max[:, t:t + 1], scale, None, ALU.mult
                                      ).then_inc(bias_ready, 1)
                if not first:
                    for t in range(TT):
                        add(c - 1, t)
                for k in range(NKEY):
                    low(c, k)
                    if first and k == 2:
                        for h in range(HT):
                            dve.wait_ge(wohi_done, h + 1)
                            dve.tensor_tensor(wo_lo[:, h, :], wo_f32[:, h, :], wo_hi[:, h, :].bitcast(F32), ALU.subtract
                                              ).then_inc(wolo_done, 1)
                    if first and k in (5, 9):
                        feed.unpack(dve, -1, GA if k == 5 else GB)
                    if not first and 1 <= k < 1 + TT:
                        statistics(c - 1, k - 1, step)
                for h in range(HT):
                    dve.wait_ge(ohi_done, HT * c + h + 1)
                    dve.tensor_tensor(o_lo[:, h, :], ps[:, 6 + h, :], o_hi[:, h, :].bitcast(F32), ALU.subtract
                                      ).then_inc(olo_done, 1)
                step.mark(dve.reciprocal(row_inv[:, :], row_sum[:, :]))
                step.wait()

            dve.wait_ge(feed.shift_in, 16)
            chunk(0, Steps(dve, step_sem, 0))
            FIRST, STEPS = TT + 1, 2 * TT + 1
            with dve.Fori(0, CHUNKS - 1) as i:
                chunk(i + 1, Steps(dve, step_sem, STEPS * i + FIRST))
            step = Steps(dve, step_sem, STEPS * (CHUNKS - 1) + FIRST)
            for t in range(TT):
                add(CHUNKS - 1, t)
                statistics(CHUNKS - 1, t, step)

        @block.tensor
        def _(pe):
            def project(j, t):
                if t >= 2:
                    pe.wait_ge(proj_added, TT * j + TT + t - 1)
                for n in range(NH):
                    for h in range(HT):
                        lhs = [o[:, h, t * P:(t + 1) * P] for o in (o_hi, o_lo)]
                        rhs = [w[:, h, n * BANK:(n + 1) * BANK] for w in (wo_hi, wo_lo)]
                        mm = three_pass(pe, ps[:, NH * (t % 2) + n, :], lhs, rhs, h == 0, h == HT - 1)
                mm.then_inc(proj_ready, 1)

            def chunk(c):
                first = isinstance(c, int)
                pe.wait_ge(q_in, 16 * c + 16)
                for t in range(TT):
                    if t == 1 and not first:
                        pe.wait_ge(olo_done, HT * c)
                    if t >= 2:
                        pe.wait_ge(exp_done, TT * c + t - 1)
                    for b in range(KB):
                        for h in range(HT):
                            lhs = [q_hl[:, s, h, t * P:(t + 1) * P] for s in range(2)]
                            rhs = [k[:, h, b * BANK:(b + 1) * BANK] for k in (k_hi, k_lo)]
                            mm = three_pass(pe, ps[:, KB * (t % 2) + b, :], lhs, rhs, h == 0, h == HT - 1)
                    mm.then_inc(scores_ready, 1)
                if not first:
                    pe.wait_ge(exp_done, TT * c + 3)
                    for t in range(TT):
                        project(c - 1, t)

                def turn(k):
                    if k == 0:
                        pe.wait_ge(exp_done, TT * c + TT)
                    if k == 2 and not first:
                        pe.wait_ge(proj_added, TT * c + 3)
                    if k >= 3:
                        pe.wait_ge(ptlo_done, NKEY * c + k - 2)
                    for t in range(TT):
                        tr = pe.transpose(ps[:, pt_bank(k), t * P:(t + 1) * P], prob[:, t, k * P:(k + 1) * P],
                                          keep["ident"][:, :])
                    tr.then_inc(pt_ready, 1)

                for k in range(3):
                    turn(k)
                for k in range(NKEY):
                    pe.wait_ge(ptlo_done, NKEY * c + k + 1)
                    for h in range(HT):
                        lhs = [v[:, k, h * P:(h + 1) * P] for v in (v_hi, v_lo)]
                        rhs = [pt[:, k % RING, :] for pt in (pt_hi, pt_lo)]
                        mm = three_pass(pe, ps[:, 6 + h, :], lhs, rhs, k == 0, k == NKEY - 1)
                    mm.then_inc(pv_done if k < NKEY - 1 else o_ready, 1)
                    if k + 3 < NKEY:
                        turn(k + 3)

            pe.wait_ge(keep["const"], 3)
            chunk(0)
            pe.wait_ge(wolo_done, HT)
            with pe.Fori(0, CHUNKS - 1) as i:
                chunk(i + 1)
            for k in range(EARLY):
                if k % 2 == 0:
                    pe.wait_ge(feed.x0_in[k // 2], 16)
                if k == 2:
                    pe.wait_ge(olo_done, HT * CHUNKS)
                    for t in range(TT):
                        project(CHUNKS - 1, t)
                transpose_quad(pe, keep, ps[:, x0_bank(k), :], feed.x0_tiles[k // 2], k % 2
                               ).then_inc(feed.xt_ready, 1)


DN0, DN1, GA, GB, UA, UB = range(6)
UNITS = 6
GATES = {GA: (0, 0), GB: (0, 1), UA: (1, 0), UB: (1, 1)}
SZ_SLOT = (1, 2, 0, 1, 2, 0)
SZ_FIRST, SZ_PAIR = (128, 64, 64), (128, 80, 80)
SZ_WITH = (16, 16, 64, 80, 80, 128)
EARLY = 4
PRO = 4


def unit(g, u):
    return g * UNITS + (PRO + u)


class Feed:

    def __init__(self, nc, d, keep, sem):
        self.d, self.keep = d, keep
        words = ROW_DOWN * 3 + UNIT * 2 + PAIR * 2 + HID * 2 + 2 * HC * BANK + 2 * KT + 8 + 8
        self.start = (nc.sbuf_usable_end - 4 * words) // 32 * 32 - 32
        m = Map(nc, self.start)
        sz2 = m.put("f_sz2", [P, ROW_DOWN], F32)
        self.start_b = m.at
        sz = m.put("f_sz", [P, 2, ROW_DOWN], F32)
        self.sz = [sz[:, 0, :], sz[:, 1, :], sz2[:, :]]
        self.wt = m.put("f_wt", [P, 2, UNIT], F32)
        self.q_in = m.put("f_q_in", [P, 2, PAIR], I32)
        self.q_dn = m.put("f_q_dn", [P, 2, HID], I32)
        self.silu = m.put("f_silu", [P, 2 * HC, BANK], F32)
        self.x_ring = self.silu[:, :, :].rearrange("p (s n) t -> p s (n t)", s=2)
        self.cur_in = m.put("f_cur_in", [P, 2, KT], I32)
        self.cur_dn = m.put("f_cur_dn", [P, 2], I32)
        self.shift = m.put("f_shift", [P, 1], I32)
        weights = keep["end_const"] + 4 * (2 * KT * HALF + HTT * HID)
        self.x0_at = [weights + 4 * words for words in (KT * PAIR, 3 * KT * PAIR, 4 * KT * PAIR)]
        later = [Map(nc, at).put(f"f_x0_{n}", [P, 2, HID], F32) for n, at in enumerate(self.x0_at)]
        self.x0_tiles = [t[:, s, :] for t in (self.x_ring, *later) for s in range(2)]
        self.x0_in = [sem(f"f_x0_in{t}") for t in range(HTT)]
        self.shift_in = sem("f_shift_in")
        self.qin_in = [sem(f"f_qin_in{w}") for w in range(2)]
        self.qdn_in = [sem(f"f_qdn_in{t}") for t in range(2)]
        self.sz_in = [sem(f"f_sz_in{s}") for s in range(3)]
        self.ring_in = [sem(f"f_ring_in{s}") for s in range(2)]
        self.x1_out = [sem(f"b_x1_out{t}") for t in range(TT)]
        self.xt_ready = sem("f_xt_ready")
        self.row_step, self.unit_step = sem("f_row_step"), sem("f_unit_step")
        self.w_made, self.wlo_done = sem("f_w_made"), sem("f_wlo_done")
        self.qdn_src = d["q_down"].rearrange("(t r) n -> t r n", r=P // PACK)
        self.x1_tiles = d["x1_scratch"].rearrange("(h n p) c -> h n p c", h=HALVES, p=P)

    def load_in(self, sp, w, blk):
        sp.dma_start(self.q_in[:, w, :], self.d[("q_gate", "q_up")[w]][blk]).then_inc(self.qin_in[w], 16)

    def load_dn(self, sp, t, blk):
        src = self.qdn_src[2 * blk + t].unsqueeze(1).to_broadcast([P // PACK, PACK, HID])
        sp.dma_start(self.q_dn[:, t, :], src).then_inc(self.qdn_in[t], 16)

    def load_x0(self, sp, t):
        sp.dma_start(self.x0_tiles[t], self.x1_tiles[0, t]).then_inc(self.x0_in[t], 16)

    def load_ring(self, sp, h, t):
        sp.dma_start(self.x_ring[:, t % 2, :], self.x1_tiles[h, t]).then_inc(self.ring_in[t % 2], 16)

    def first_rows(self, pool, step):
        for w, name in enumerate(("gate", "up")):
            ins = pool.tensor_copy(self.cur_in[:, w, :], self.keep["row_" + name])
        step.mark(ins)

    def gather(self, pool, u):
        slot = SZ_SLOT[u]
        if u in GATES:
            w, quad = GATES[u]
            table, width = self.d[("table_gate", "table_up")[w]], ROW_IN
            rows = [self.cur_in[:, w, k:k + 1] for k in range(QUAD * quad, QUAD * quad + QUAD)]
        else:
            table, width, rows = self.d["table_down"], ROW_DOWN, [self.cur_dn[:, u:u + 1]]
        for i, row in enumerate(rows):
            pool.indirect_dma_start(out=self.sz[slot][:, i * width:(i + 1) * width], out_offset=None, in_=table,
                                    in_offset=bass.IndirectOffsetOnAxis(ap=row, axis=0)).then_inc(self.sz_in[slot], 16)

    def unpack(self, dve, g, u):
        n, slot, s = unit(g, u), u % 2, SZ_SLOT[u]
        step = Steps(dve, self.unit_step, n * 2)
        val, sz = self.wt[:, slot, :], self.sz[s]
        if not (isinstance(n, int) and n < 2):
            dve.wait_ge(self.wlo_done, n - 1)
        if u in GATES:
            w, quad = GATES[u]
            dve.wait_ge(self.qin_in[w], (g + 1) * 16 + 16)
            for i in range(QUAD):
                ins = dve.tensor_scalar(val.bitcast(I32)[:, i * PAIR:(i + 1) * PAIR], self.q_in[:, w, :],
                                        BITS * (QUAD * quad + i), 15, ALU.logical_shift_right, ALU.bitwise_and)
            ints = val.bitcast(I32).rearrange("p (i n) -> p i n", i=QUAD)
            val = val.rearrange("p (i n) -> p i n", i=QUAD)
            scale = sz.rearrange("p (i w) -> p i w", i=QUAD)[:, :, 0:PAIR]
            zero = sz.bitcast(BF16).rearrange("p (i w) -> p i w", i=QUAD)[:, :, 2 * PAIR:3 * PAIR]
        else:
            dve.wait_ge(self.qdn_in[u], g * 16 + 16)
            ins = dve.tensor_scalar(val.bitcast(I32), self.q_dn[:, u, :], self.shift[:, 0:1], 15,
                                    ALU.logical_shift_right, ALU.bitwise_and)
            ints, scale, zero = val.bitcast(I32), sz[:, 0:HID], sz.bitcast(BF16)[:, 2 * HID:3 * HID]
        step.mark(ins)
        step.wait()
        dve.wait_ge(self.sz_in[s], g * SZ_PAIR[s] + (SZ_FIRST[s] + SZ_WITH[u]))
        step.mark(dve.tensor_tensor(val, ints, zero, ALU.subtract))
        step.wait()
        dve.tensor_tensor(val, val, scale, ALU.mult).then_inc(self.w_made, 1)


def phase_mlp(nc, d, ps, keep, sem, feed):
    m = Map(nc, keep["end_const"])
    x_hi, x_lo = m.put("c_x_hi", [P, KT, HALF], F32R), m.put("c_x_lo", [P, KT, HALF], F32R)
    acc = m.put("c_acc", [P, HTT, HID], F32)
    weights = m.at
    in_hi, in_lo = m.put("c_in_hi", [P, 2, KT, PAIR], F32R), m.put("c_in_lo", [P, 2, KT, PAIR], F32R)
    assert feed.x0_at == [weights + 4 * KT * PAIR, weights + 12 * KT * PAIR, m.at]
    dn_hi, dn_lo = m.put("c_dn_hi", [P, 2, HID], F32R), m.put("c_dn_lo", [P, 2, HID], F32R)
    h_hi, h_lo = m.put("c_h_hi", [P, 2, HALF], F32R), m.put("c_h_lo", [P, 2, HALF], F32R)
    stats = m.put("c_stats", [P, HTT, NH, 6], F32)
    mv, var_eps, rstd = m.put("c_mv", [P, HTT, 2], F32), m.put("c_var_eps", [P, HTT], F32), m.put("c_rstd", [P, HTT], F32)
    neg_mean = m.put("c_neg_mean", [P, HTT], F32)

    assert m.at <= feed.start
    silu, x_ring, wt = feed.silu, feed.x_ring, feed.wt
    ring_in, sz_in, row_step, unit_step, w_made, wlo_done = (
        feed.ring_in, feed.sz_in, feed.row_step, feed.unit_step, feed.w_made, feed.wlo_done)
    acc_in = [sem(f"c_acc_in{t}") for t in range(HTT)]
    out_done = [sem(f"c_out_done{t}") for t in range(HTT)]
    ln_step, eps_step, whi_done = sem("c_ln_step"), sem("c_eps_step"), sem("c_whi_done")
    xt_ready, xhi_done, xlo_done = feed.xt_ready, sem("c_xhi_done"), sem("c_xlo_done")
    gate_ready, up_ready = sem("c_gate_ready"), sem("c_up_ready")
    rest_moved = sem("c_rest_moved")
    down_ready = sem("c_down_ready")
    silu_done, h_made, hhi_done, hlo_done = sem("c_silu_done"), sem("c_h_made"), sem("c_hhi_done"), sem("c_hlo_done")
    acc_done = sem("c_acc_done")
    var_done, rstd_done, x2_done = sem("c_var_done"), sem("c_rstd_done"), sem("c_x2_done")

    BLK = 2 * HC
    DN = HTT * NH
    XT = HTT * 2
    assert BLK == 4 and DN == 16

    x1_tiles = d["x1_scratch"].rearrange("(h n p) c -> h n p c", h=HALVES, p=P)
    out_tiles = d["out"].rearrange("(h n p) c -> h n p c", h=HALVES, p=P)

    def halves(eng, body):
        for h in range(HALVES):
            with eng.Fori(0, PAIRS - 1) as p:
                body(h, p, p + h * PAIRS, False)
            body(h, PAIRS - 1, h * PAIRS + PAIRS - 1, True)
            yield h

    def shared(last, b):
        return last and b >= HC

    def more(h, last):
        return not (last and h == HALVES - 1)

    with nc.Block() as block:
        @block.sync
        def _(sp):
            def body(h, p, g, last):
                if more(h, last):
                    for t in range(2):
                        sp.wait_ge(unit_step, unit(g, DN0 + t) * 2 + 1)
                        feed.load_dn(sp, t, p + 1)
                    sp.wait_ge(unit_step, unit(g, GB) * 2 + 1)
                    feed.load_in(sp, 0, p + 2)
                    if last:
                        for t in range(HTT):
                            if t < 2:
                                sp.wait_ge(hlo_done, g * BLK + BLK + 2 * (t + 1))
                            else:
                                sp.wait_ge(xt_ready, XT * (h + 1) + 2 * (t - 2) + 2)
                            feed.load_ring(sp, h + 1, t)
                    sp.wait_ge(unit_step, unit(g, UB) * 2 + 1)
                    feed.load_in(sp, 1, p + 2)

            sp.wait_ge(unit_step, 2 * 1 + 1)
            feed.load_in(sp, 0, 1)
            sp.wait_ge(unit_step, 2 * 3 + 1)
            feed.load_in(sp, 1, 1)
            for t in range(HTT):
                sp.dma_start(acc[:, t, :], x1_tiles[0, t]).then_inc(acc_in[t], 16)
            for t in range(TT):
                sp.wait_ge(feed.x1_out[t], 16 * (CHUNKS + 1))
            for h in halves(sp, body):
                for t in range(HTT):
                    sp.wait_ge(x2_done, HTT * h + t + 1)
                    sp.dma_start(out_tiles[h, t], acc[:, t, :]).then_inc(out_done[t], 16)
                if h < HALVES - 1:
                    g = PAIRS * (h + 1)
                    sp.wait_ge(sz_in[1], g * SZ_PAIR[1] + SZ_FIRST[1] + SZ_WITH[GB])
                for t in range(HTT):
                    sp.wait_ge(out_done[t], 16 * (h + 1))
                    if h < HALVES - 1:
                        sp.dma_start(acc[:, t, :], x1_tiles[h + 1, t]).then_inc(acc_in[t], 16)

        @block.gpsimd
        def _(pool):
            def body(h, p, g, last):
                def fetch(u):
                    wait_apart(pool, keep, w_made, unit(g, u) - 2)
                    feed.gather(pool, u)

                step = Steps(pool, row_step, g * 2 + (h + 1))
                for s in (1, 2):
                    pool.wait_ge(sz_in[s], g * SZ_PAIR[s] + SZ_FIRST[s])
                step.mark(pool.tensor_copy(feed.cur_dn[:, :], keep["row_down"][:, bass.ts(p, 2)]))
                step.wait()
                fetch(DN0)
                fetch(DN1)
                wait_apart(pool, keep, sz_in[0], g * SZ_PAIR[0] + SZ_FIRST[0])
                step.mark(pool.tensor_scalar(feed.cur_in[:, :, :], feed.cur_in[:, :, :], 1.0, None, ALU.add))
                step.wait()
                if more(h, last):
                    for u in (GA, GB, UA, UB):
                        fetch(u)

            feed.gather(pool, UA)
            pool.wait_ge(w_made, 1)
            feed.gather(pool, UB)
            for h in halves(pool, body):
                if h < HALVES - 1:
                    for s in range(3):
                        pool.wait_ge(sz_in[s], (h + 1) * PAIRS * SZ_PAIR[s] + SZ_FIRST[s])
                    feed.first_rows(pool, Steps(pool, row_step, 2 * PAIRS * (h + 1) + h + 1))
                step = Steps(pool, eps_step, 3 * HTT * h)
                for t in range(HTT):
                    pool.wait_ge(var_done, HTT * h + t + 1)
                    rstd_steps(pool, mv[:, t, :], var_eps[:, t:t + 1], rstd[:, t:t + 1], neg_mean[:, t:t + 1],
                               keep["minus_half"][:, 0:1], step, rstd_done)

        @block.scalar
        def _(act):
            def in_hi_unit(n, w, half):
                out = in_hi[:, w, QUAD * half:QUAD * (half + 1), :].rearrange("p i n -> p (i n)")
                act.wait_ge(w_made, n + 1)
                act.activation(out, wt[:, half, :], ACT.Copy).then_inc(whi_done, 1)

            def x_hi_quad(h, k, bank):
                act.wait_ge(xt_ready, XT * h + k + 1)
                t, quad = k // 2, k % 2
                act.activation(x_hi[:, QUAD * quad:QUAD * (quad + 1), t * P:(t + 1) * P],
                               ps[:, bank, :].rearrange("p (i t) -> p i t", t=P), ACT.Copy).then_inc(xhi_done, 1)

            def body(h, p, g, last):
                if last:
                    act.wait_ge(wlo_done, unit(g, DN0))
                    act.activation(in_hi[:, 1, :, P + P // 2:PAIR], in_hi[:, 0, :, P:P + P // 2].bitcast(F32), ACT.Copy
                                   ).then_inc(rest_moved, 1)
                gates = g * BLK - h * HC

                def silu_block(b):
                    if shared(last, b):
                        act.wait_ge(up_ready, g * BLK + b + 1)
                    else:
                        act.wait_ge(gate_ready, gates + b + 1)
                    act.wait_ge(hlo_done, g * BLK + b + 1)
                    if shared(last, b):
                        act.activation(silu[0:REST, b, :], ps[P // 2:P // 2 + REST, 4 + b, :], ACT.Silu
                                       ).then_inc(silu_done, 1)
                    else:
                        act.activation(silu[:, b, :], ps[:, b, :], ACT.Silu).then_inc(silu_done, 1)

                for b in range(HC if last else BLK):
                    silu_block(b)
                    if b < 2:
                        act.wait_ge(w_made, unit(g, DN0 + b) + 1)
                        act.wait_ge(down_ready, g * DN + DN)
                        act.activation(dn_hi[:, b, :], wt[:, b, :], ACT.Copy).then_inc(whi_done, 1)

                def h_high(b):
                    act.wait_ge(h_made, g * BLK + BLK + b + 1)
                    rows = slice(0, REST if shared(last, b) else P)
                    act.activation(h_hi[rows, b // HC, (b % HC) * BANK:(b % HC + 1) * BANK], silu[rows, b, :], ACT.Copy
                                   ).then_inc(hhi_done, 1)

                if more(h, last):
                    act.wait_ge(gate_ready, gates + (HC if last else BLK))
                    in_hi_unit(unit(g, GA), 0, 0)
                h_high(0)
                if more(h, last):
                    in_hi_unit(unit(g, GB), 0, 1)
                for b in range(1, BLK):
                    if shared(last, b):
                        silu_block(b)
                    h_high(b)
                turned = last and h < HALVES - 1
                if last:
                    for t in range(HTT + 1):
                        if turned and t < HTT:
                            for k in (2 * t, 2 * t + 1):
                                x_hi_quad(h + 1, k, x_bank(k))
                        if t:
                            act.wait_ge(rstd_done, HTT * h + t)
                            act.activation(acc[:, t - 1, :], acc[:, t - 1, :], ACT.Identity, scale=rstd[:, t - 1:t],
                                           bias=neg_mean[:, t - 1:t]).then_inc(x2_done, 1)
                if more(h, last):
                    act.wait_ge(up_ready, g * BLK + BLK)
                    in_hi_unit(unit(g, UA), 1, 0)
                    in_hi_unit(unit(g, UB), 1, 1)

            act.sem_inc(h_made, BLK)
            act.sem_inc(hlo_done, BLK)
            for k in range(XT):
                if k == 8:
                    in_hi_unit(0, 0, 0)
                    in_hi_unit(1, 0, 1)
                x_hi_quad(0, k, x0_bank(k))
            in_hi_unit(2, 1, 0)
            in_hi_unit(3, 1, 1)
            for t in range(TT):
                act.wait_ge(feed.x1_out[t], 16 * (CHUNKS + 1))
            for h in halves(act, body):
                pass

        @block.vector
        def _(dve):
            def w_low(n, slot, hi, lo):
                dve.wait_ge(whi_done, n + 1)
                dve.tensor_tensor(lo, wt[:, slot, :], hi.bitcast(F32), ALU.subtract).then_inc(wlo_done, 1)

            def in_low(n, w, half):
                hi, lo = (t[:, w, QUAD * half:QUAD * (half + 1), :].rearrange("p i n -> p (i n)") for t in (in_hi, in_lo))
                w_low(n, half, hi, lo)

            def x_low_quad(h, k, bank):
                dve.wait_ge(xhi_done, XT * h + k + 1)
                t, quad = k // 2, k % 2
                hi, lo = (x[:, QUAD * quad:QUAD * (quad + 1), t * P:(t + 1) * P] for x in (x_hi, x_lo))
                dve.tensor_tensor(lo, ps[:, bank, :].rearrange("p (i t) -> p i t", t=P), hi.bitcast(F32), ALU.subtract
                                  ).then_inc(xlo_done, 1)

            def body(h, p, g, last):
                turned = last and h < HALVES - 1
                step = Steps(dve, ln_step, HTT * h)

                def h_make(b):
                    dve.wait_ge(up_ready, g * BLK + b + 1)
                    dve.wait_ge(silu_done, g * BLK + b + 1)
                    rows = slice(0, REST if shared(last, b) else P)
                    dve.tensor_tensor(silu[rows, b, :], silu[rows, b, :], ps[rows, 4 + b, :], ALU.mult
                                      ).then_inc(h_made, 1)

                def h_low(b):
                    dve.wait_ge(hhi_done, g * BLK + b + 1)
                    rows = slice(0, REST if shared(last, b) else P)
                    hi, lo = (t[rows, b // HC, (b % HC) * BANK:(b % HC + 1) * BANK] for t in (h_hi, h_lo))
                    dve.tensor_tensor(lo, silu[rows, b, :], hi.bitcast(F32), ALU.subtract).then_inc(hlo_done, 1)

                def add(n):
                    t, b = n // NH, n % NH
                    part = acc[:, t, b * BANK:(b + 1) * BANK]
                    dve.wait_ge(down_ready, g * DN + DN + n + 1)
                    if b == 0:
                        dve.wait_ge(acc_in[t], 16 * (h + 1))
                    bank = (4 * t + b) % 8 if turned else n % 8
                    dve.tensor_tensor(part, ps[:, bank, :], part, ALU.add).then_inc(acc_done, 1)

                def add_tile(t):
                    for n in range(NH * t, NH * t + NH):
                        add(n)
                    if turned:
                        for k in (2 * t, 2 * t + 1):
                            x_low_quad(h + 1, k, x_bank(k))
                    if last:
                        dve.wait_ge(acc_done, g * DN + DN + NH * (t + 1))
                        layer_norm_steps(dve, keep, acc[:, t, :], stats[:, t, :, :], mv[:, t, :], step, var_done)

                if last:
                    dve.wait_ge(wlo_done, unit(g, DN0))
                    dve.tensor_copy(in_lo[:, 1, :, P + P // 2:PAIR], in_lo[:, 0, :, P:P + P // 2].bitcast(F32)
                                    ).then_inc(rest_moved, 1)
                feed.unpack(dve, g, DN0)
                feed.unpack(dve, g, DN1)
                w_low(unit(g, DN0), 0, dn_hi[:, 0, :], dn_lo[:, 0, :])
                w_low(unit(g, DN1), 1, dn_hi[:, 1, :], dn_lo[:, 1, :])
                if more(h, last):
                    feed.unpack(dve, g, GA)
                h_make(0)
                if more(h, last):
                    in_low(unit(g, GA), 0, 0)
                    feed.unpack(dve, g, GB)
                h_make(1)
                h_low(0)
                if more(h, last):
                    in_low(unit(g, GB), 0, 1)
                h_low(1)
                h_make(2)
                h_low(2)
                h_make(3)
                h_low(3)
                if more(h, last):
                    if turned:
                        for t in range(HTT):
                            add_tile(t)
                    feed.unpack(dve, g, UA)
                    if not turned:
                        add_tile(0)
                        add_tile(1)
                    in_low(unit(g, UA), 1, 0)
                    feed.unpack(dve, g, UB)
                    if not turned:
                        add_tile(2)
                        add_tile(3)
                    in_low(unit(g, UB), 1, 1)
                    for t in range(4, 0 if turned else HTT):
                        add_tile(t)
                else:
                    for t in range(HTT):
                        add_tile(t)

            dve.sem_inc(acc_done, DN)
            for k in range(XT):
                if k == 8:
                    in_low(0, 0, 0)
                    in_low(1, 0, 1)
                x_low_quad(0, k, x0_bank(k))
            feed.unpack(dve, -1, UA)
            in_low(2, 1, 0)
            feed.unpack(dve, -1, UB)
            in_low(3, 1, 1)
            for h in halves(dve, body):
                pass

        @block.tensor
        def _(pe):
            def turn(h, k, bank):
                t, quad = k // 2, k % 2
                if quad == 0:
                    if h == 0:
                        pe.wait_ge(feed.x0_in[t], 16)
                    else:
                        pe.wait_ge(ring_in[t % 2], 16 * (HTT // 2 * (h - 1) + t // 2 + 1))
                src = feed.x0_tiles[t] if h == 0 else x_ring[:, t % 2, :]
                transpose_quad(pe, keep, ps[:, bank, :], src, quad).then_inc(xt_ready, 1)

            def body(h, p, g, last):
                turned = last and h < HALVES - 1
                def product(w, j, c, ready, bank):
                    pe.wait_ge(acc_done, g * DN + 8 + bank + 1)
                    for i in range(KT):
                        if i == 0 and j == 0 and w == 0:
                            pe.wait_ge(xlo_done, XT * h + 2 * TT * (c + 1))
                        if j == 0 and c == 0 and i % QUAD == 0:
                            pe.wait_ge(wlo_done, g * UNITS + 2 * w + i // QUAD + 1)
                        cols, toks = slice(j * P, (j + 1) * P), slice(c * BANK, (c + 1) * BANK)
                        mm = three_pass(pe, ps[:, bank, :], (in_hi[:, w, i, cols], in_lo[:, w, i, cols]),
                                        (x_hi[:, i, toks], x_lo[:, i, toks]), i == 0, i == KT - 1)
                    mm.then_inc(ready, 1)

                for w, ready in ((0, gate_ready), (1, up_ready)):
                    for j in range(1 if last else 2):
                        for c in range(HC):
                            product(w, j, c, ready, 4 * w + HC * j + c)
                if last:
                    pe.wait_ge(rest_moved, 2 * (h + 1))
                    for c in range(HC):
                        product(1, 1, c, up_ready, 4 + HC + c)
                pe.wait_ge(wlo_done, unit(g, DN1) + 1)
                for t in range(HTT):
                    if t % TT == 0:
                        pe.wait_ge(hlo_done, g * BLK + BLK + HC + t // TT + 1)
                    for b in range(NH):
                        n, e = NH * t + b, 4 * t + b if turned else NH * t + b
                        bank = e % 8
                        if e < 4:
                            if not shared(last, bank):
                                pe.wait_ge(silu_done, g * BLK + bank + 1)
                        elif e < 8:
                            pe.wait_ge(h_made, g * BLK + BLK + bank - 4 + 1)
                        else:
                            pe.wait_ge(acc_done, g * DN + DN + (n - 4 if turned else n - 8) + 1)
                        for j in range(2):
                            toks, cols = slice(t * P, (t + 1) * P), slice(b * BANK, (b + 1) * BANK)
                            rows = slice(0, REST if shared(last, HC * j) else P)
                            mm = three_pass(pe, ps[:, bank, :], (h_hi[rows, j, toks], h_lo[rows, j, toks]),
                                            (dn_hi[rows, j, cols], dn_lo[rows, j, cols]), j == 0, j == 1)
                        mm.then_inc(down_ready, 1)
                    if turned:
                        for k in (2 * t, 2 * t + 1):
                            if t == 1:
                                pe.wait_ge(h_made, g * BLK + BLK + x_bank(k) - 4 + 1)
                            elif t:
                                pe.wait_ge(xlo_done, XT * (h + 1) + k - 4 + 1)
                            turn(h + 1, k, x_bank(k))

            pe.sem_inc(down_ready, DN)
            for k in range(EARLY, XT):
                if k >= 8:
                    pe.wait_ge(xlo_done, (k - 8 if k < 12 else k - 4) + 1)
                turn(0, k, x0_bank(k))
            for h in halves(pe, body):
                if h < HALVES - 1:
                    pe.wait_ge(acc_done, DN * PAIRS * (h + 1) + 14)
                    pe.wait_ge(xlo_done, XT * (h + 1) + 14)


def x0_bank(k):
    return (k + 4) % 8 if k < 8 else 4 + k % 4


def x_bank(k):
    return (4 * (k // 2) + 2 + k % 2) % 8


def build(nc, d, out):
    d["out"] = out
    sems = {}

    def sem(name):
        sems[name] = nc.alloc_semaphore(name)
        return sems[name]

    d["q_scratch"] = nc.dram_tensor("q_scratch", (CHUNKS, P, 2 * HT * CHUNK), F32).ap()
    d["x1_scratch"] = nc.dram_tensor("x1_scratch", (TOKENS, HID), F32).ap()
    d["table_gate"] = nc.dram_tensor("table_gate", (GROUPS_IN * BLOCKS, ROW_IN), F32).ap()
    d["table_up"] = nc.dram_tensor("table_up", (GROUPS_IN * BLOCKS, ROW_IN), F32).ap()
    d["table_down"] = nc.dram_tensor("table_down", (GROUPS_DOWN, ROW_DOWN), F32).ap()

    m = Map(nc, SBUF_FIRST)
    ident, minus_half = m.put("ident", [P, P], F32), m.put("minus_half", [P, 1], F32)
    keep = {"ident": ident, "minus_half": minus_half, "const": sem("const")}
    for name, n in (("gate", KT), ("up", KT), ("down", 2 * PAIRS)):
        keep["row_" + name] = m.put("row_" + name, [P, n], I32)[:, :]
    keep["end_const"] = m.at
    for name in ("k_hi", "k_lo"):
        keep[name] = m.put(name, [P, HT, TOKENS], F32R)
    for name in ("v_hi", "v_lo"):
        keep[name] = m.put(name, [P, NKEY, HEAD], F32R)
    keep["end"] = m.at
    keep["q_hl"] = m.put("b_q_hl", [P, 2, HT, CHUNK], F32R)
    keep["q_in"], keep["end_q"] = sem("b_q_in"), m.at
    with nc.psum_tensor("ps", [P, 8, BANK], F32) as ps:
        phase_qkv(nc, d, ps, keep, sem)
        feed = Feed(nc, d, keep, sem)
        phase_attention(nc, d, ps, keep, sem, feed)
        phase_mlp(nc, d, ps, keep, sem, feed)


def _blocks(a, wrap):
    out = np.zeros((P, PAIRS, PAIR), a.dtype)
    out.reshape(P, INTER_PAD)[:, :INTER] = a
    out = out.transpose(1, 0, 2)
    return np.ascontiguousarray(np.concatenate([out, out[:wrap]]))


def _wide(a, n, axis):
    shape = list(a.shape)
    shape[axis] = n
    out = np.zeros(shape, a.dtype)
    out[tuple(slice(0, s) for s in a.shape)] = a
    return out


def kernel(**inputs):
    import concourse.bacc as bacc
    from concourse.bass_utils import run_bass_kernel_spmd

    a = {k.removeprefix("L0_"): np.asarray(v) for k, v in inputs.items()}
    x = a["attn_x"].reshape(TOKENS, HID)
    q_down = _wide(a["ffn_down_qweight"], (PAIRS + 1) * PAIR // PACK, 0)
    q_down[PAIRS * PAIR // PACK:] = q_down[:PAIR // PACK]
    arrays = {
        "x": x,
        "xT": np.ascontiguousarray(x.T),
        "Wqkv": a["attn_Wqkv"],
        "bias_qk": np.ascontiguousarray(a["attn_bqkv"][:2 * HEAD].reshape(2 * HT, P).T),
        "bias_v": a["attn_bqkv"][2 * HEAD:].reshape(1, HEAD),
        "Wo": a["attn_Wo"],
        "bo": a["attn_bo"].reshape(1, HID),
        "q_gate": _blocks(a["ffn_gate_qweight"], 2),
        "q_up": _blocks(a["ffn_up_qweight"], 2),
        "q_down": q_down,
        "scales_gate": _wide(a["ffn_gate_scales"], INTER_PAD, 1),
        "scales_up": _wide(a["ffn_up_scales"], INTER_PAD, 1),
        "scales_down": a["ffn_down_scales"],
        "zeros_gate": _wide(a["ffn_gate_qzeros"], INTER_PAD // PACK, 1),
        "zeros_up": _wide(a["ffn_up_qzeros"], INTER_PAD // PACK, 1),
        "zeros_down": a["ffn_down_qzeros"],
        "g_idx_gate": a["ffn_gate_g_idx"].reshape(P, KT),
        "g_idx_up": a["ffn_up_g_idx"].reshape(P, KT),
        "g_idx_down": np.ascontiguousarray(_wide(a["ffn_down_g_idx"], INTER_PAD, 0).reshape(2 * PAIRS, P).T),
        "shift": np.tile(np.arange(0, 32, BITS, dtype=np.int32), P // PACK).reshape(P, 1),
    }
    arrays = {k: np.ascontiguousarray(v) for k, v in arrays.items()}

    nc = bacc.Bacc("TRN2", target_bir_lowering=False, num_devices=1)
    d = {k: nc.dram_tensor(k, v.shape, mybir.dt.from_np(v.dtype), kind="ExternalInput").ap() for k, v in arrays.items()}
    out = nc.dram_tensor("out", (TOKENS, HID), F32, kind="ExternalOutput").ap()
    build(nc, d, out)
    r = run_bass_kernel_spmd(nc, [arrays], core_ids=[0])
    return r.results[0]["out"].reshape(1, TOKENS, HID)
```
